# Optimizing a Trainium2 kernel written in Bass

```python
import numpy as np
import jax
import jax.numpy as jnp

def _softmax(x, axis=-1):
    return jax.nn.softmax(x, axis=axis)

def _gelu(x):
    return jax.nn.gelu(x, approximate=True)

def _silu(x):
    return jax.nn.silu(x)

def _sigmoid(x):
    return jax.nn.sigmoid(x)

def _layernorm(x, axis=-1, eps=1e-05):
    m = jnp.mean(x, axis=axis, keepdims=True)
    v = jnp.var(x, axis=axis, keepdims=True)
    return (x - m) / jnp.sqrt(v + eps)

def _scatter_add(tgt, idx, src, axis=0):
    return tgt.at[idx].add(src)

def _segment_sum(src, seg, n):
    return jax.ops.segment_sum(src, seg, n)
kernel_name = 'mk_conv_preact_d2_conv_nhwc512_r2_6c1608'

def setup_inputs(seed: int=0):
    np.random.seed(seed)
    _w = jnp.asarray

    def _rec_inputs():
        import jax
        import jax.numpy as jnp
        _gk = jax.random.key(seed)
        x = -0.0003929 + 0.9999 * jax.random.normal(jax.random.fold_in(_gk, 1), (8, 32, 32, 256), jnp.float32)
        return x
    x = _rec_inputs()

    def _L0_conv_setup():
        import jax, jax.numpy as jnp
        import numpy as np
        D_MODEL = 256
        N_HEAD = 16
        HEAD_DIM = D_MODEL // N_HEAD
        SCALE = HEAD_DIM ** (-0.5)
        SIZE = (32, 32)
        WINDOW = (8, 8)
        SHIFT = (4, 4)
        WS = WINDOW[0] * WINDOW[1]
        NW = SIZE[0] // WINDOW[0] * (SIZE[1] // WINDOW[1])

        def _rel_pos_index(window):
            w0, w1 = window
            coords = np.stack(np.meshgrid(np.arange(w0), np.arange(w1), indexing='ij')).reshape(2, -1)
            rel = (coords[:, :, None] - coords[:, None, :]).transpose(1, 2, 0)
            rel[:, :, 0] += w0 - 1
            rel[:, :, 1] += w1 - 1
            rel[:, :, 0] *= 2 * w1 - 1
            return rel.sum(-1)

        def _shift_mask(size, window, shift):
            H, W = size
            w0, w1 = window
            s0, s1 = shift
            img = np.zeros((H, W))
            cnt = 0
            h_slices = (slice(0, -w0), slice(-w0, -s0), slice(-s0, None)) if s0 > 0 else (slice(None),)
            w_slices = (slice(0, -w1), slice(-w1, -s1), slice(-s1, None)) if s1 > 0 else (slice(None),)
            for hs in h_slices:
                for ws_ in w_slices:
                    img[hs, ws_] = cnt
                    cnt += 1
            win = img.reshape(H // w0, w0, W // w1, w1).transpose(0, 2, 1, 3).reshape(-1, w0 * w1)
            return (win[:, None, :] != win[:, :, None]).astype(np.float32)
        REL_IDX = jnp.asarray(_rel_pos_index(WINDOW))
        MASK = jnp.asarray(-100.0 * _shift_mask(SIZE, WINDOW, SHIFT))
        key = jax.random.key(seed)
        k1, k2, k3, k4 = jax.random.split(key, 4)
        x = jax.random.normal(k1, (8, SIZE[0], SIZE[1], D_MODEL), dtype=jnp.float32)
        qkv_w = jax.random.normal(k2, (3 * D_MODEL, D_MODEL), dtype=jnp.float32) * D_MODEL ** (-0.5)
        qkv_b = jax.random.normal(k3, (3 * D_MODEL,), dtype=jnp.float32) * 0.02
        bias_table = jax.random.normal(k4, ((2 * WINDOW[0] - 1) * (2 * WINDOW[1] - 1), N_HEAD), dtype=jnp.float32) * 0.02
        return {'x': x, 'qkv_w': qkv_w, 'qkv_b': qkv_b, 'bias_table': bias_table}
    _L0_conv_all = _L0_conv_setup()
    _L0_conv_in = {k: v for k, v in _L0_conv_all.items() if k in ('qkv_w', 'qkv_b', 'bias_table')}
    del _L0_conv_all

    def _L1_conv_setup():
        import jax, jax.numpy as jnp
        import numpy as np
        TAU = 2.0
        V_THRESHOLD = 1.0
        V_RESET = 0.0
        ATAN_ALPHA = 2.0
        T, B, L, D_IN, D_OUT = (16, 32, 64, 256, 256)

        @jax.custom_vjp
        def atan_spike(x):
            return (x >= 0.0).astype(x.dtype)

        def _atan_spike_fwd(x):
            return (atan_spike(x), x)

        def _atan_spike_bwd(x, g):
            grad = ATAN_ALPHA / 2.0 / (1.0 + (jnp.pi / 2.0 * ATAN_ALPHA * x) ** 2)
            return (g * grad,)
        atan_spike.defvjp(_atan_spike_fwd, _atan_spike_bwd)

        def lif_multistep(h):

            def step(v, x_t):
                v = v + (x_t - (v - V_RESET)) / TAU
                s = atan_spike(v - V_THRESHOLD)
                s_d = jax.lax.stop_gradient(s)
                v = V_RESET * s_d + v * (1.0 - s_d)
                return (v, s)
            v0 = jnp.zeros_like(h[0])
            _, spikes = jax.lax.scan(step, v0, h)
            return spikes
        key = jax.random.key(seed)
        kx, kw, kb = jax.random.split(key, 3)
        x = jax.random.normal(kx, (T, B, L, D_IN), dtype=jnp.float32)
        bound = 1.0 / np.sqrt(D_IN)
        W = jax.random.uniform(kw, (D_OUT, D_IN), minval=-bound, maxval=bound, dtype=jnp.float32)
        b = jax.random.uniform(kb, (D_OUT,), minval=-bound, maxval=bound, dtype=jnp.float32)
        return {'x': x, 'W': W, 'b': b}
    _L1_conv_all = _L1_conv_setup()
    _L1_conv_in = {k: v for k, v in _L1_conv_all.items() if k in ('W', 'b')}
    del _L1_conv_all
    return {'x': x, 'L0_conv_qkv_w': _L0_conv_in['qkv_w'], 'L0_conv_qkv_b': _L0_conv_in['qkv_b'], 'L0_conv_bias_table': _L0_conv_in['bias_table'], 'L1_conv_W': _L1_conv_in['W'], 'L1_conv_b': _L1_conv_in['b']}

def reference(x, L0_conv_qkv_w, L0_conv_qkv_b, L0_conv_bias_table, L1_conv_W, L1_conv_b):
    import jax
    import jax.numpy as jnp

    def _L0_conv_ref(x, qkv_w, qkv_b, bias_table):
        import jax, jax.numpy as jnp
        import numpy as np
        D_MODEL = 256
        N_HEAD = 16
        HEAD_DIM = D_MODEL // N_HEAD
        SCALE = HEAD_DIM ** (-0.5)
        SIZE = (32, 32)
        WINDOW = (8, 8)
        SHIFT = (4, 4)
        WS = WINDOW[0] * WINDOW[1]
        NW = SIZE[0] // WINDOW[0] * (SIZE[1] // WINDOW[1])

        def _rel_pos_index(window):
            w0, w1 = window
            coords = np.stack(np.meshgrid(np.arange(w0), np.arange(w1), indexing='ij')).reshape(2, -1)
            rel = (coords[:, :, None] - coords[:, None, :]).transpose(1, 2, 0)
            rel[:, :, 0] += w0 - 1
            rel[:, :, 1] += w1 - 1
            rel[:, :, 0] *= 2 * w1 - 1
            return rel.sum(-1)

        def _shift_mask(size, window, shift):
            H, W = size
            w0, w1 = window
            s0, s1 = shift
            img = np.zeros((H, W))
            cnt = 0
            h_slices = (slice(0, -w0), slice(-w0, -s0), slice(-s0, None)) if s0 > 0 else (slice(None),)
            w_slices = (slice(0, -w1), slice(-w1, -s1), slice(-s1, None)) if s1 > 0 else (slice(None),)
            for hs in h_slices:
                for ws_ in w_slices:
                    img[hs, ws_] = cnt
                    cnt += 1
            win = img.reshape(H // w0, w0, W // w1, w1).transpose(0, 2, 1, 3).reshape(-1, w0 * w1)
            return (win[:, None, :] != win[:, :, None]).astype(np.float32)
        REL_IDX = jnp.asarray(_rel_pos_index(WINDOW))
        MASK = jnp.asarray(-100.0 * _shift_mask(SIZE, WINDOW, SHIFT))
        n, H, W, c = x.shape
        w0, w1 = WINDOW
        part = x.reshape(n, H // w0, w0, W // w1, w1, c)
        part = part.transpose(0, 1, 3, 2, 4, 5).reshape(n * NW, WS, c)
        qkv = (part @ qkv_w.T + qkv_b).reshape(n * NW, WS, 3, N_HEAD, HEAD_DIM)
        q, k, v = (qkv[:, :, 0] * SCALE, qkv[:, :, 1], qkv[:, :, 2])
        attn = jnp.einsum('wihd,wjhd->whij', q, k)
        bias = bias_table[REL_IDX].transpose(2, 0, 1)
        attn = attn.reshape(n, NW, N_HEAD, WS, WS) + bias[None, None] + MASK[None, :, None]
        attn = jax.nn.softmax(attn, axis=-1).reshape(n * NW, N_HEAD, WS, WS)
        out = jnp.einsum('whij,wjhd->wihd', attn, v).reshape(n * NW, WS, c)
        out = out.reshape(n, H // w0, W // w1, w0, w1, c)
        return out.transpose(0, 1, 3, 2, 4, 5).reshape(n, H, W, c)

    def _L1_conv_ref(x, W, b):
        import jax, jax.numpy as jnp
        import numpy as np
        TAU = 2.0
        V_THRESHOLD = 1.0
        V_RESET = 0.0
        ATAN_ALPHA = 2.0
        T, B, L, D_IN, D_OUT = (16, 32, 64, 256, 256)

        @jax.custom_vjp
        def atan_spike(x):
            return (x >= 0.0).astype(x.dtype)

        def _atan_spike_fwd(x):
            return (atan_spike(x), x)

        def _atan_spike_bwd(x, g):
            grad = ATAN_ALPHA / 2.0 / (1.0 + (jnp.pi / 2.0 * ATAN_ALPHA * x) ** 2)
            return (g * grad,)
        atan_spike.defvjp(_atan_spike_fwd, _atan_spike_bwd)

        def lif_multistep(h):

            def step(v, x_t):
                v = v + (x_t - (v - V_RESET)) / TAU
                s = atan_spike(v - V_THRESHOLD)
                s_d = jax.lax.stop_gradient(s)
                v = V_RESET * s_d + v * (1.0 - s_d)
                return (v, s)
            v0 = jnp.zeros_like(h[0])
            _, spikes = jax.lax.scan(step, v0, h)
            return spikes
        h = jnp.einsum('tbld,hd->tblh', x, W) + b
        return lif_multistep(h)

    def _gn(v, G=32, eps=1e-05):
        B_, H_, W_, C_ = v.shape
        g = v.reshape(B_, H_, W_, G, C_ // G)
        m = jnp.mean(g, axis=(1, 2, 4), keepdims=True)
        s = jnp.var(g, axis=(1, 2, 4), keepdims=True)
        return ((g - m) / jnp.sqrt(s + eps)).reshape(v.shape)

    def _ln_c(v, eps=1e-06):
        m = jnp.mean(v, axis=-1, keepdims=True)
        s = jnp.var(v, axis=-1, keepdims=True)
        return (v - m) / jnp.sqrt(s + eps)

    def _ln_t(v, eps=1e-05):
        m = jnp.mean(v, axis=-1, keepdims=True)
        s = jnp.var(v, axis=-1, keepdims=True)
        return (v - m) / jnp.sqrt(s + eps)

    def _to_tokens(v):
        B_, H_, W_, C_ = v.shape
        return v.reshape(B_, H_ * W_, C_)

    def _from_tokens(t, like):
        return t.reshape(like.shape)
    x = x + _L0_conv_ref(_gn(x), L0_conv_qkv_w, L0_conv_qkv_b, L0_conv_bias_table)
    x = x + _L1_conv_ref(_gn(x), L1_conv_W, L1_conv_b)
    return x

_drawn_inputs = setup_inputs


def setup_inputs(seed=0):
    import zlib

    import numpy as np

    out = dict(_drawn_inputs(seed))
    spreads = {}
    factors = {'L0_conv_bias_table': 8.0, 'L1_conv_b': 3.846}
    for name, (base, spread) in spreads.items():
        noise = np.random.default_rng([zlib.crc32(name.encode()), seed]).standard_normal(out[name].shape)
        drawn = base * np.exp(spread * noise) if base else spread * noise
        out[name] = jnp.asarray(drawn.astype(out[name].dtype))
    for name, factor in factors.items():
        out[name] = (out[name] * factor).astype(out[name].dtype)
    return out
```

```python
import concourse.bass as bass
from concourse import mybir
from contextlib import ExitStack


def swin_attention_then_lif_kernel(nc, x, qkv_w, qkv_b, bias_table, lif_w, lif_b, out):
    f32, f32r = mybir.dt.float32, mybir.dt.float32r
    f16, bf16, i32 = mybir.dt.float16, mybir.dt.bfloat16, mybir.dt.int32
    ALU = mybir.AluOpType
    ACT = mybir.ActivationFunctionType
    AX = mybir.AxisListType

    SAMPLES, HEIGHT, WIDTH, C = x.shape
    WIN = 8
    WS = WIN * WIN
    HEADS = bias_table.shape[1]
    D = C // HEADS
    HALVES = C // 128
    WROWS = HEIGHT // WIN
    WCOLS = WIDTH // WIN
    ROWS = SAMPLES * WROWS
    PAIRS = ROWS * 2
    ROWTOK = WCOLS * WS
    QUADS = 4
    QK_SCALE = float(D) ** -0.5
    TAU = 2.0
    EPS = 1e-5
    GROUP = C // 32
    MASK = -100.0
    OUTS = 3 * C + C
    PV_N = 2 * (D + 1)
    WIN_N = QUADS * PV_N

    x_windows = x.rearrange("s (y yi) (wx xi) c -> (s y) wx yi xi c", yi=WIN, xi=WIN)
    x_rows = x.rearrange("s (y a yi) w c -> (s y) (yi w) a c", a=2, yi=WIN // 2)
    out_rows = out.rearrange("s (y a yi) w c -> (s y) (yi w) a c", a=2, yi=WIN // 2)

    ctx = ExitStack()
    with ctx:
        def sb(name, shape, dt):
            return ctx.enter_context(nc.sbuf_tensor(name, shape, dt))

        def sem(name):
            return ctx.enter_context(nc.semaphore(name))

        xc = sb("xc", [128, ROWS, HALVES * ROWTOK], f32)
        w_hi = sb("w_hi", [128, HALVES, OUTS], f32r)
        w_lo = sb("w_lo", [128, HALVES, OUTS], f32r)
        b_row = sb("b_row", [128, OUTS], f32r)
        ones_r = sb("ones_r", [128, ROWTOK], f32r)
        vbias = sb("vbias", [128, C], f32)
        ident = sb("ident", [128, 128], f32)
        ident_r = sb("ident_r", [128, 128], f32r)
        ident_b = sb("ident_b", [128, 128], bf16)
        group_avg = sb("group_avg", [128, 128], f32)
        parity_mask = sb("parity_mask", [128, 2], f32)
        pick_max = sb("pick_max", [128, 2 * QUADS, 128], bf16)
        bias_hi = sb("bias_hi", [128, 4, 512], f32r)
        bias_lo = sb("bias_lo", [128, 4, 512], f32r)
        bias_q = sb("bias_q", [128, 4, 512], f32r)
        stats = sb("stats", [128, ROWS, HALVES, 6], f32)
        moments = sb("moments", [128, SAMPLES * HALVES, 2], f32)
        neg_mean = sb("neg_mean", [128, (SAMPLES + 1) * HALVES], f32)
        rstd = sb("rstd", [128, (SAMPLES + 1) * HALVES], f32)
        tiny = [sb(f"tiny{i}", [128, SAMPLES * HALVES], f32) for i in range(6)]

        wstage = sb("wstage", [128, OUTS // 128, C], f32)
        bias_sum = wstage[:, :, :].rearrange("p t c -> p (t c)").rearrange("p (v n) -> p v n", v=4)
        bias_raw = sb("bias_raw", [128, WIN * WIN * HEADS], f32)
        flip = sb("flip", [128, 128], f32)
        masks = sb("masks", [128, 4, WS], f32)
        bits = sb("bits", [128, 4], i32)
        flags = sb("flags", [128, 3], f32)
        xstage = sb("xstage", [128, 4, 2 * C], f32)
        xn = sb("xn", [128, HALVES * ROWTOK], f32)
        xn_hi = [sb(f"xn_hi{i}", [128, HALVES * ROWTOK], f32r) for i in range(2)]
        xn_lo = [sb(f"xn_lo{i}", [128, HALVES * ROWTOK], f32r) for i in range(2)]
        q_hi = [sb(f"q_hi{i}", [128, HALVES, WCOLS, QUADS, WS], f16) for i in range(2)]
        q_lo = [sb(f"q_lo{i}", [128, HALVES, WCOLS, QUADS, WS], f16) for i in range(2)]
        k_hi = [sb(f"k_hi{i}", [128, HALVES, WCOLS, 2, WS], f16) for i in range(2)]
        k_lo = [sb(f"k_lo{i}", [128, HALVES, WCOLS, 2, WS], f16) for i in range(2)]
        v_hi = [sb(f"v_hi{i}", [128, HALVES, 2, QUADS, 2, D + 1], f16) for i in range(4)]
        v_lo = [sb(f"v_lo{i}", [128, HALVES, 2, QUADS, 2, D + 1], f16) for i in range(4)]
        probs = sb("probs", [128, 2 * QUADS, 2, WS], f32)
        p_hi = [sb(f"p_hi{i}", [128, 2 * QUADS, 2, WS], f16) for i in range(2)]
        p_lo = [sb(f"p_lo{i}", [128, 2 * QUADS, 2, WS], f16) for i in range(2)]
        neg_max = sb("neg_max", [128, 16], f32)
        max_split = [sb(f"max_split{i}", [128, 32], bf16) for i in range(2)]
        max_rows = [sb(f"max_rows{i}", [128, 128], bf16) for i in range(2)]
        b_raw = probs[:, :, :, :].rearrange("p g w i -> p (g w i)")
        recip = sb("recip", [128, HALVES, 2 * QUADS], f32)
        attn = sb("attn", [128, HALVES, 2 * QUADS, D], f32)
        x1 = [sb(f"x1_{i}", [128, C], f32) for i in range(2)]
        lif_x = [sb(f"lif_x{i}", [128, HALVES * ROWTOK], f32) for i in range(2)]
        charged = [sb(f"charged{i}", [128, 2 * C], f32) for i in range(2)]
        membrane = sb("membrane", [128, 2 * C], f32)

        max_ps, score_ps, pv_ps, proj_ps = [
            ctx.enter_context(nc.psum_tensor(name, [128, 2, 512], f32))
            for name in ("max_ps", "score_ps", "pv_ps", "proj_ps")]
        banks = [t[:, j, :] for t in (max_ps, score_ps, pv_ps, proj_ps) for j in range(2)]

        w_loaded = sem("w_loaded")
        tab_loaded = sem("tab_loaded")
        b_loaded = sem("b_loaded")
        vb_loaded = sem("vb_loaded")
        const_step = sem("const_step")
        setup_pe = sem("setup_pe")
        setup_act = sem("setup_act")
        setup_dve = sem("setup_dve")
        mask_step = sem("mask_step")
        in_loaded = [sem(f"in_loaded{i}") for i in range(4)]
        in_turned = [sem(f"in_turned{i}") for i in range(4)]
        in_kept = [sem(f"in_kept{i}") for i in range(4)]
        stats_done = sem("stats_done")
        norm_pe = sem("norm_pe")
        norm_act = sem("norm_act")
        norm_dve = sem("norm_dve")
        norm_ready = sem("norm_ready")
        centred = sem("centred")
        xn_done = sem("xn_done")
        xn_hi_done = sem("xn_hi_done")
        xn_lo_done = sem("xn_lo_done")
        q_ps_done = sem("q_ps_done")
        k_ps_done = sem("k_ps_done")
        v_ps_done = sem("v_ps_done")
        q_hi_done = sem("q_hi_done")
        k_hi_done = sem("k_hi_done")
        v_hi_done = sem("v_hi_done")
        q_lo_done = sem("q_lo_done")
        k_lo_done = sem("k_lo_done")
        v_lo_done = sem("v_lo_done")
        max_ps_done = sem("max_ps_done")
        neg_max_done = sem("neg_max_done")
        max_hi_done = sem("max_hi_done")
        max_split_done = sem("max_split_done")
        max_turned = sem("max_turned")
        max_rows_done = sem("max_rows_done")
        score_ps_done = sem("score_ps_done")
        p_hi_done = sem("p_hi_done")
        p_lo_done = sem("p_lo_done")
        pv_ps_done = sem("pv_ps_done")
        recip_done = sem("recip_done")
        attn_done = sem("attn_done")
        res_loaded = [sem(f"res_loaded{i}") for i in range(4)]
        res_done = sem("res_done")
        x1_done = sem("x1_done")
        x1_turned = sem("x1_turned")
        x1_kept = sem("x1_kept")
        lif_loaded = [sem(f"lif_loaded{i}") for i in range(2)]
        h_ps_done = sem("h_ps_done")
        lif_xt_done = sem("lif_xt_done")
        charge_done = sem("charge_done")
        reset_done = sem("reset_done")
        spike_done = sem("spike_done")
        stored = [sem(f"stored{i}") for i in range(4)]

        def wait(eng, s, value):
            if not isinstance(value, int) or value > 0:
                eng.wait_ge(s, value)

        def one(tensor, row):
            return tensor[:, bass.ds(row, 1), :].rearrange("p a n -> p (a n)")

        def sample_of(row):
            return row // WROWS if isinstance(row, int) else row >> (WROWS.bit_length() - 1)

        def run(eng, body):
            for k in range(BODY):
                body(k, k // 2, k)
            with eng.Fori(1, LAST) as i:
                for k in range(BODY):
                    body(i * BODY + k, i * 2 + k // 2, k)
            for k in range(BODY):
                body(LAST * BODY + k, LAST * 2 + k // 2, k)

        def is_first(n, lag):
            return isinstance(n, int) and n < lag

        def is_last_row(row, ahead=1):
            return isinstance(row, int) and row + ahead >= ROWS

        BODY = 4
        LAST = PAIRS // BODY - 1
        W_TILES = OUTS // 128
        W_SCALES = [QK_SCALE, 1.0, 1.0, 1.0 / TAU]

        NORMS = SAMPLES * HALVES
        NORM_STEPS = 9
        SETUP_DVE = 6
        SETUP_ACT = 14

        def v_part(p, w, e):
            return proj_ps[w * WS:(w + 1) * WS, 0, p * C:(p + 1) * C]\
                .rearrange("p (h g e d) -> p h g e d", h=HALVES, g=QUADS, e=2)[:, :, :, e, :]

        block = ctx.enter_context(nc.Block())

        @block.sync
        def _(sp):
            sp.dma_start(wstage[:, 0:3 * C // 128, :], qkv_w.rearrange("(t p) c -> p t c", p=128)).then_inc(w_loaded, 16)
            sp.dma_start(wstage[:, 3 * C // 128:W_TILES, :], lif_w.rearrange("(t p) c -> p t c", p=128)).then_inc(w_loaded, 16)
            def load_sample(s):
                for slot in range(4):
                    wait(sp, in_turned[slot], s)
                    sp.dma_start(xstage[:, slot, :].rearrange("p (a c) -> p a c", a=2),
                                 x_rows[bass.ds(s * WROWS + slot, 1)].rearrange("r p a c -> p (r a) c"))\
                      .then_inc(in_loaded[slot], 16)

            load_sample(0)
            with sp.Fori(1, SAMPLES) as s:
                load_sample(s)

            def load_residual(row, p, slot):
                for w in range(2):
                    sp.dma_start(xstage[w * WS:(w + 1) * WS, slot, 0:C],
                                 x_windows[bass.ds(row, 1), 2 * p + w]).then_inc(res_loaded[slot], 16)

            for slot in range(4):
                sp.wait_ge(in_turned[slot], SAMPLES)
                load_residual(slot // 2, slot % 2, slot)
            with sp.Fori(1, LAST + 1) as i:
                for k in range(BODY):
                    sp.wait_ge(x1_done, i * BODY + (k - 3))
                    load_residual(i * 2 + k // 2, k % 2, k)

            sp.wait_ge(norm_ready, 2)

            def store(y, t):
                slot = t % 4
                sp.wait_ge(spike_done, y * SAMPLES + (t + 1))
                sp.dma_start(out_rows[bass.ds(y + t * WROWS, 1)].rearrange("r p a c -> p (r a) c"),
                             xstage[:, slot, :].rearrange("p (a c) -> p a c", a=2)).then_inc(stored[slot], 16)

            def lif_units(y):
                for t in range(SAMPLES):
                    wait(sp, lif_xt_done, y * SAMPLES + (t - 1))
                    sp.dma_start(lif_x[t % 2][:, :], one(xc, y + t * WROWS)).then_inc(lif_loaded[t % 2], 16)
                    if t > 0:
                        store(y, t - 1)
                store(y, SAMPLES - 1)

            lif_units(0)
            with sp.Fori(1, WROWS) as y:
                lif_units(y)
            for slot in range(4):
                sp.wait_ge(stored[slot], 16 * SAMPLES * WROWS // 4)

        @block.gpsimd
        def _(pool):
            pool.memset(ident[:, :], 0.0).then_inc(const_step, 1)
            pool.memset(flip[:, :], 0.0)
            pool.memset(group_avg[:, :], 1.0 / GROUP).then_inc(const_step, 1)
            pool.iota(bits[:, 0:1], pattern=[[0, 1]], base=0, channel_multiplier=1).then_inc(const_step, 1)
            pool.wait_ge(const_step, 3)
            pool.affine_select(out=ident[:, :], in_=ident[:, :], compare_op=ALU.not_equal, fill=1.0, base=0,
                               pattern=[[-1, 128]], channel_multiplier=1)
            pool.affine_select(out=flip[:, :], in_=flip[:, :], compare_op=ALU.not_equal, fill=1.0, base=-127,
                               pattern=[[1, 128]], channel_multiplier=1).then_inc(const_step, 1)
            grp = group_avg[:, :].rearrange("p (g e) -> p g e", e=GROUP)
            pool.affine_select(out=grp, in_=grp, compare_op=ALU.is_ge, fill=0.0, base=0,
                               pattern=[[-GROUP, 128 // GROUP], [0, GROUP]], channel_multiplier=1).then_inc(const_step, 1)
            pool.wait_ge(const_step, 5)
            pool.affine_select(out=grp, in_=grp, compare_op=ALU.is_ge, fill=0.0, base=GROUP - 1,
                               pattern=[[GROUP, 128 // GROUP], [0, GROUP]], channel_multiplier=-1).then_inc(const_step, 1)
            for buf in q_hi + q_lo + k_hi + k_lo:
                pool.memset(buf[:, :, :, :, :], 0.0)
            for buf in v_hi + v_lo:
                pool.memset(buf[:, :, :, :, :, :], 0.0)
            for buf in max_rows:
                zeroed = pool.memset(buf[:, :], 0.0)
            zeroed.then_inc(const_step, 1)
            pool.wait_ge(const_step, 7)
            for buf in v_hi:
                for e in range(2):
                    for h in range(HALVES):
                        ones = pool.memset(buf[e * WS:(e + 1) * WS, h, :, :, e, D:D + 1], 1.0)
            ones.then_inc(const_step, 1)
            pool.wait_ge(const_step, 8)

            def normalise(row, sample, layer, done):
                pool.wait_ge(norm_ready, layer)
                wait(pool, xn_lo_done, done)
                def wide(column):
                    return column[:, bass.ds(sample * HALVES, HALVES)].unsqueeze(2).to_broadcast([128, HALVES, ROWTOK])

                halves = xn[:, :].rearrange("p (h n) -> p h n", h=HALVES)
                pool.tensor_tensor(halves, one(xc, row).rearrange("p (h n) -> p h n", h=HALVES), wide(neg_mean), ALU.add)\
                    .then_inc(centred, 1)
                pool.wait_ge(centred, done + 1)
                last = pool.tensor_tensor(halves, halves, wide(rstd), ALU.mult)
                last.then_inc(xn_done, 1)

            def low_part(slot, done):
                pool.wait_ge(xn_hi_done, done)
                pool.tensor_tensor(xn_lo[slot][:, :], xn[:, :], xn_hi[slot][:, :].bitcast(f32), ALU.subtract)\
                    .then_inc(xn_lo_done, 1)

            for r in range(2):
                normalise(r, 0, 1, r)
                low_part(r, r + 1)
            pool.wait_ge(vb_loaded, 16)

            def pair(n, row, k):
                p = k % 2
                if not is_last_row(row, 2):
                    if p == 0:
                        normalise(row + 2, sample_of(row + 2), 1, row + 2)
                    else:
                        low_part(k // 2, row + 3)
                pool.wait_ge(res_loaded[k], (n // 4 + 1) * 32 if isinstance(n, int) else (n + (BODY - k)) * (32 // BODY))
                pool.tensor_tensor(xstage[:, k, 0:C], xstage[:, k, 0:C], vbias[:, :], ALU.add).then_inc(res_done, 1)
                wait(pool, pv_ps_done, n - 1)
                for w in range(2):
                    pool.wait_ge(p_hi_done, n * 2 + (w + 1))
                    pool.tensor_tensor(p_lo[p][:, :, w, :], probs[:, :, w, :], p_hi[p][:, :, w, :], ALU.subtract)\
                        .then_inc(p_lo_done, 1)

            run(pool, pair)

            def lif_units(y):
                for t in range(SAMPLES):
                    normalise(y + t * WROWS, t, 2, y * SAMPLES + (ROWS + t))
                    low_part(t % 2, y * SAMPLES + (ROWS + t + 1))

            lif_units(0)
            with pool.Fori(1, WROWS) as y:
                lif_units(y)

        @block.scalar
        def _(act):
            span = 2 * WIN - 1
            for e in range(2):
                for yj in range(WIN):
                    src = bass.AP(tensor=bias_table.tensor, offset=yj * span * HEADS,
                                  ap=[[HEADS, WIN], [span * HEADS, WIN], [1, WIN * HEADS]])
                    act.dma_start(bias_raw[e * WS + yj * WIN:e * WS + (yj + 1) * WIN, :], src).then_inc(tab_loaded, 16)
            act.dma_start(vbias[:, :], qkv_b[2 * C:3 * C].partition_broadcast(128)).then_inc(vb_loaded, 16)
            act.wait_ge(setup_dve, 1)
            for r in (0, 32):
                act.dma_start(b_raw[r:r + 1, 0:3 * C], qkv_b.rearrange("(o c) -> o c", o=1)).then_inc(b_loaded, 16)
                act.dma_start(b_raw[r:r + 1, 3 * C:OUTS], lif_b.rearrange("(o c) -> o c", o=1)).then_inc(b_loaded, 16)
            for b in range(4):
                act.wait_ge(setup_pe, b + 1)
                for j in range(2):
                    kind = (b % 2) * 2 + j
                    act.activation(w_hi[:, b // 2, kind * C:(kind + 1) * C], banks[b][:, j * C:(j + 1) * C], ACT.Copy,
                                   scale=W_SCALES[kind]).then_inc(setup_act, 1)
            act.wait_ge(setup_dve, 3)
            act.activation(b_row[:, :], b_raw, ACT.Copy).then_inc(setup_act, 1)
            act.wait_ge(setup_dve, 4)
            act.activation(bias_hi[:, :, :], bias_sum, ACT.Copy).then_inc(setup_act, 1)
            for v in range(4):
                act.wait_ge(setup_pe, 6 + v)
                act.activation(bias_q[:, v, :], banks[4 + v], ACT.Copy).then_inc(setup_act, 1)

            with act.Fori(0, SAMPLES) as s:
                for slot in range(4):
                    act.wait_ge(in_turned[slot], s + 1)
                    for h in range(HALVES):
                        src = banks[slot][:, h * ROWTOK:(h + 1) * ROWTOK].rearrange("p (y w x) -> p w y x", y=WIN, w=WCOLS)
                        dst = one(xc, s * WROWS + slot)[:, h * ROWTOK:(h + 1) * ROWTOK]\
                            .rearrange("p (w y x) -> p w y x", y=WIN, w=WCOLS)
                        last = act.activation(dst, src, ACT.Copy)
                    last.then_inc(in_kept[slot], 1)

            def square_root(done):
                act.wait_ge(norm_dve, done)
                act.activation(tiny[5][:, :], tiny[4][:, :], ACT.Sqrt).then_inc(norm_act, 1)

            def xn_high(slot, done):
                act.wait_ge(xn_done, done)
                act.activation(xn_hi[slot][:, :], xn[:, :], ACT.Copy).then_inc(xn_hi_done, 1)

            def q_high(slot, done):
                act.wait_ge(q_ps_done, done)
                for g in range(QUADS):
                    rows = slice(32 * g, 32 * g + 32)
                    last = act.activation(q_hi[slot][rows, :, :, g, :].rearrange("p h w i -> p (h w) i"),
                                          proj_ps[rows, 0, :].rearrange("p (n i) -> p n i", i=WS), ACT.Copy)
                last.then_inc(q_hi_done, 1)

            def k_high(slot, done):
                act.wait_ge(k_ps_done, done)
                for e in range(2):
                    last = act.activation(k_hi[slot][:, :, :, e, :].rearrange("p h w j -> p (h w) j"),
                                          proj_ps[:, 1, :].rearrange("p (n j) -> p n j", j=WS), ACT.Copy,
                                          scale=parity_mask[:, e:e + 1])
                last.then_inc(k_hi_done, 1)

            def v_high(slot, done):
                act.wait_ge(v_ps_done, done)
                for p in range(2):
                    for w in range(2):
                        for e in range(2):
                            last = act.activation(v_hi[2 * slot + p][e * WS:(e + 1) * WS, :, w, :, e, 0:D],
                                                  v_part(p, w, e), ACT.Copy)
                last.then_inc(v_hi_done, 1)

            square_root(NORM_STEPS - 4)
            xn_high(0, 1)
            act.wait_ge(setup_dve, SETUP_DVE)
            act.wait_ge(const_step, 8)
            q_high(0, 1)
            k_high(0, 1)
            v_high(0, 1)
            xn_high(1, 2)

            def keep_x1(m, row, k):
                act.wait_ge(x1_turned, m + 1)
                for h in range(HALVES):
                    src = proj_ps[:, 1, h * 128:(h + 1) * 128].rearrange("p (w y x) -> p w y x", w=2, y=WIN)
                    dst = one(xc, row)[:, h * ROWTOK:(h + 1) * ROWTOK]\
                        .rearrange("p (y w x) -> p w y x", y=WIN, w=WCOLS)[:, 2 * (k % 2):2 * (k % 2) + 2]
                    last = act.activation(dst, src, ACT.Copy)
                last.then_inc(x1_kept, 1)

            def pair(n, row, k):
                p = k % 2
                nxt = 1 - k // 2
                if not is_last_row(row):
                    if p == 0:
                        q_high(nxt, row + 2)
                        k_high(nxt, row + 2)
                    else:
                        v_high(nxt, row + 2)
                if p == 1 and not is_last_row(row, 2):
                    xn_high(k // 2, row + 3)
                act.wait_ge(max_turned, n + 1)
                act.activation(max_rows[p][0:32, :], max_ps[:, 0, :].bitcast(bf16)[0:32, 0:128], ACT.Copy)\
                    .then_inc(max_rows_done, 1)
                wait(act, pv_ps_done, n - 1)
                for w in range(2):
                    wait(act, p_lo_done, n * 2 + (w - 1))
                    act.wait_ge(score_ps_done, n * 2 + (w + 1))
                    scores = score_ps[:, w, :].rearrange("p (g i) -> p g i", i=WS)
                    act.activation(probs[:, :, w, :], scores, ACT.Exp)
                    act.activation(p_hi[p][:, :, w, :], scores, ACT.Exp).then_inc(p_hi_done, 1)
                if not is_first(n, 2):
                    keep_x1(n - 2, row - 1, k)

            run(act, pair)
            keep_x1(PAIRS - 2, ROWS - 1, 0)
            keep_x1(PAIRS - 1, ROWS - 1, 1)
            square_root(2 * NORM_STEPS - 4)

            def lif_units(y):
                for t in range(SAMPLES):
                    wait(act, h_ps_done, y * SAMPLES + (t - 1))
                    xn_high(t % 2, y * SAMPLES + (ROWS + t + 1))

            lif_units(0)
            with act.Fori(1, WROWS) as y:
                lif_units(y)

        @block.vector
        def _(dve):
            dve.memset(b_raw, 0.0).then_inc(setup_dve, 1)
            dve.memset(ones_r[:, :].bitcast(f32), 1.0)
            dve.memset(masks[:, :, :], 0.0).then_inc(setup_dve, 1)
            dve.wait_ge(b_loaded, 64)
            for r in (0, 32):
                dve.tensor_scalar(b_raw[r:r + 1, 0:C], b_raw[r:r + 1, 0:C], QK_SCALE, None, ALU.mult)
                last = dve.tensor_scalar(b_raw[r:r + 1, 3 * C:OUTS], b_raw[r:r + 1, 3 * C:OUTS], 1.0 / TAU, None, ALU.mult)
            last.then_inc(setup_dve, 1)
            dve.wait_ge(const_step, 4)
            for j, bit in enumerate((4, 32, 16)):
                last = dve.tensor_scalar(bits[:, j + 1:j + 2], bits[:, 0:1], bit, None, ALU.bitwise_and)
            last.then_inc(mask_step, 1)
            dve.wait_ge(setup_dve, 2)
            dve.memset(masks[:, 1, :].rearrange("p (y x) -> p y x", x=WIN)[:, :, WIN // 2:WIN], 1.0)
            dve.memset(masks[:, 2, WS // 2:WS], 1.0).then_inc(mask_step, 1)
            dve.wait_ge(mask_step, 2)
            dve.tensor_scalar(flags[:, :], bits[:, 1:4], 0.0, None, ALU.is_gt).then_inc(mask_step, 1)
            dve.wait_ge(mask_step, 3)
            for v in (1, 2):
                last = dve.tensor_scalar(masks[:, v, :], masks[:, v, :], flags[:, v - 1:v], MASK, ALU.not_equal, ALU.mult)
            dve.tensor_copy(parity_mask[:, 1:2], flags[:, 2:3])
            dve.tensor_scalar(parity_mask[:, 0:1], flags[:, 2:3], -1.0, 1.0, ALU.mult, ALU.add).then_inc(mask_step, 1)
            dve.wait_ge(mask_step, 4)
            dve.tensor_tensor(masks[:, 3, :], masks[:, 1, :], masks[:, 2, :], ALU.min).then_inc(mask_step, 1)
            dve.tensor_copy(ident_r[:, :], ident[:, :])
            dve.tensor_copy(ident_b[:, :], ident[:, :]).then_inc(mask_step, 1)
            dve.wait_ge(mask_step, 6)
            dve.tensor_tensor(pick_max[:, :, :].rearrange("p v (e j) -> p (v e) j", e=2),
                              ident_b[:, 0:16].unsqueeze(2).to_broadcast([128, 16, WS]),
                              ident_b[:, 16:32].unsqueeze(2).to_broadcast([128, 16, WS]), ALU.add)
            dve.wait_ge(setup_pe, 5)
            for v in range(4):
                for e in range(2):
                    half = slice(e * WS, (e + 1) * WS)
                    last = dve.tensor_tensor(
                        bias_sum[half, v, :].rearrange("p (g i) -> p g i", i=WS),
                        pv_ps[half, :, :].rearrange("p b (n h) -> p h (b n)", h=HEADS)[:, e:HEADS:2, :],
                        masks[half, v:v + 1, :].to_broadcast([WS, 2 * QUADS, WS]), ALU.add)
            last.then_inc(setup_dve, 1)
            for b in range(4):
                dve.wait_ge(setup_act, 2 * b + 2)
                for j in range(2):
                    kind = (b % 2) * 2 + j
                    cols = slice(kind * C, (kind + 1) * C)
                    last = dve.scalar_tensor_tensor(w_lo[:, b // 2, cols], banks[b][:, j * C:(j + 1) * C], W_SCALES[kind],
                                                    w_hi[:, b // 2, cols].bitcast(f32), ALU.mult, ALU.subtract)
            last.then_inc(setup_dve, 1)
            dve.wait_ge(setup_act, 9)
            dve.tensor_tensor(b_row[32:33, :], b_raw[32:33, :], b_row[32:33, :].bitcast(f32), ALU.subtract)
            dve.wait_ge(setup_act, 10)
            dve.tensor_tensor(bias_lo[:, :, :], bias_sum, bias_hi[:, :, :].bitcast(f32), ALU.subtract).then_inc(setup_dve, 1)

            def row_stats(row):
                for h in range(HALVES):
                    last = dve.bn_stats(stats[:, bass.ds(row, 1), h, :].rearrange("p a n -> p (a n)"),
                                        one(xc, row)[:, h * ROWTOK:(h + 1) * ROWTOK])
                return last

            with dve.Fori(0, SAMPLES) as s:
                for slot in range(4):
                    dve.wait_ge(in_kept[slot], s + 1)
                    row_stats(s * WROWS + slot).then_inc(stats_done, 1)

            def norm_constants(layer):
                count = [(layer - 1) * NORM_STEPS]

                def step(instruction):
                    instruction.then_inc(norm_dve, 1)
                    count[0] += 1
                    dve.wait_ge(norm_dve, count[0])

                dve.wait_ge(stats_done, layer * ROWS)
                for s in range(SAMPLES):
                    for h in range(HALVES):
                        last = dve.bn_aggr(moments[:, s * HALVES + h, :], stats[:, s * WROWS:(s + 1) * WROWS, h, :])
                step(last)
                dve.wait_ge(norm_pe, 2 * layer - 1)
                dve.tensor_scalar(neg_mean[:, 0:NORMS], proj_ps[:, 0, 0:NORMS], -1.0, None, ALU.mult)
                step(dve.tensor_tensor(tiny[0][:, :], moments[:, :, 0], proj_ps[:, 0, 0:NORMS], ALU.subtract))
                step(dve.tensor_tensor(tiny[1][:, :], tiny[0][:, :], tiny[0][:, :], ALU.mult))
                step(dve.tensor_tensor(tiny[2][:, :], tiny[1][:, :], moments[:, :, 1], ALU.add))
                dve.wait_ge(norm_pe, 2 * layer)
                step(dve.tensor_scalar(tiny[4][:, :], proj_ps[:, 0, NORMS:2 * NORMS], EPS, None, ALU.add))
                dve.wait_ge(norm_act, layer)
                step(dve.reciprocal(tiny[0][:, :], tiny[5][:, :]))
                step(dve.tensor_tensor(tiny[1][:, :], tiny[0][:, :], tiny[4][:, :], ALU.mult))
                step(dve.tensor_tensor(tiny[2][:, :], tiny[1][:, :], tiny[5][:, :], ALU.add))
                step(dve.tensor_scalar(tiny[3][:, :], tiny[2][:, :], 0.5, None, ALU.mult))
                dve.reciprocal(rstd[:, 0:NORMS], tiny[3][:, :]).then_inc(norm_ready, 1)
                assert count[0] == layer * NORM_STEPS

            norm_constants(1)

            def q_low(slot, done):
                dve.wait_ge(q_hi_done, done)
                for g in range(QUADS):
                    rows = slice(32 * g, 32 * g + 32)
                    last = dve.tensor_tensor(q_lo[slot][rows, :, :, g, :].rearrange("p h w i -> p (h w) i"),
                                             proj_ps[rows, 0, :].rearrange("p (n i) -> p n i", i=WS),
                                             q_hi[slot][rows, :, :, g, :].rearrange("p h w i -> p (h w) i"), ALU.subtract)
                last.then_inc(q_lo_done, 1)

            def k_low(slot, done):
                dve.wait_ge(k_hi_done, done)
                for e in range(2):
                    last = dve.scalar_tensor_tensor(k_lo[slot][:, :, :, e, :].rearrange("p h w j -> p (h w) j"),
                                                    proj_ps[:, 1, :].rearrange("p (n j) -> p n j", j=WS),
                                                    parity_mask[:, e:e + 1],
                                                    k_hi[slot][:, :, :, e, :].rearrange("p h w j -> p (h w) j"),
                                                    ALU.mult, ALU.subtract)
                last.then_inc(k_lo_done, 1)

            def v_low(slot, done):
                dve.wait_ge(v_hi_done, done)
                for p in range(2):
                    for w in range(2):
                        for e in range(2):
                            rows = slice(e * WS, (e + 1) * WS)
                            last = dve.tensor_tensor(v_lo[2 * slot + p][rows, :, w, :, e, 0:D], v_part(p, w, e),
                                                     v_hi[2 * slot + p][rows, :, w, :, e, 0:D], ALU.subtract)
                last.then_inc(v_lo_done, 1)

            def maxima(n, p):
                dve.wait_ge(max_ps_done, n + 1)
                dve.tensor_reduce(neg_max[:, :], max_ps[:, :, :].rearrange("p w (n j) -> p (w n) j", j=WS), AX.X, ALU.max,
                                  negate=True).then_inc(neg_max_done, 1)
                dve.wait_ge(neg_max_done, n + 1)
                dve.tensor_copy(max_split[p][:, 0:16], neg_max[:, :]).then_inc(max_hi_done, 1)
                dve.wait_ge(max_hi_done, n + 1)
                dve.tensor_tensor(max_split[p][:, 16:32], neg_max[:, :], max_split[p][:, 0:16], ALU.subtract)\
                    .then_inc(max_split_done, 1)

            def attention_out(m, k):
                dve.wait_ge(pv_ps_done, m + 1)

                def window(w):
                    return pv_ps[w * WS:(w + 1) * WS, :, w * WIN_N:(w + 1) * WIN_N].rearrange("p h (n d) -> p h n d", d=D + 1)

                for w in range(2):
                    last = dve.reciprocal(recip[w * WS:(w + 1) * WS, :, :], window(w)[:, :, :, D])
                last.then_inc(recip_done, 1)
                dve.wait_ge(recip_done, m + 1)
                for w in range(2):
                    rows = slice(w * WS, (w + 1) * WS)
                    last = dve.tensor_tensor(attn[rows, :, :, :], window(w)[:, :, :, 0:D],
                                             recip[rows, :, :].unsqueeze(3).to_broadcast([WS, HALVES, 2 * QUADS, D]),
                                             ALU.mult)
                last.then_inc(attn_done, 1)
                dve.wait_ge(attn_done, m + 1)
                dve.wait_ge(res_done, m + 1)
                wait(dve, x1_turned, m - 1)
                dve.tensor_tensor(x1[k % 2][:, :], attn[:, :, :, :].rearrange("p h n d -> p (h n d)"), xstage[:, k, 0:C],
                                  ALU.add).then_inc(x1_done, 1)

            dve.wait_ge(const_step, 8)
            q_low(0, 1)
            k_low(0, 1)
            v_low(0, 1)
            maxima(0, 0)

            def pair(n, row, k):
                p = k % 2
                nxt = 1 - k // 2
                if not is_last_row(row):
                    if p == 0:
                        q_low(nxt, row + 2)
                        k_low(nxt, row + 2)
                    else:
                        v_low(nxt, row + 2)
                if not is_first(n, 1):
                    attention_out(n - 1, (k - 1) % 4)
                if not (isinstance(n, int) and n + 1 >= PAIRS):
                    maxima(n + 1, 1 - p)
                if p == 0 and not is_first(n, 4):
                    dve.wait_ge(x1_kept, n - 2)
                    row_stats(row - 2).then_inc(stats_done, 1)

            run(dve, pair)
            attention_out(PAIRS - 1, 3)
            for back in (2, 1):
                dve.wait_ge(x1_kept, PAIRS + 2 - 2 * back)
                row_stats(ROWS - back).then_inc(stats_done, 1)
            norm_constants(2)

            def lif_units(y):
                for t in range(SAMPLES):
                    m = y * SAMPLES + t
                    h_ps = banks[t % 2]
                    dve.wait_ge(h_ps_done, m + 1)
                    wait(dve, spike_done, y * SAMPLES + (t - 1))
                    if t == 0:
                        dve.tensor_copy(charged[t % 2][:, :], h_ps).then_inc(charge_done, 1)
                    else:
                        dve.wait_ge(reset_done, m)
                        dve.scalar_tensor_tensor(charged[t % 2][:, :], membrane[:, :], 1.0 - 1.0 / TAU, h_ps, ALU.mult, ALU.add)\
                           .then_inc(charge_done, 1)
                    dve.wait_ge(charge_done, m + 1)
                    dve.scalar_tensor_tensor(membrane[:, :], charged[t % 2][:, :], 1.0, charged[t % 2][:, :], ALU.is_lt, ALU.mult)\
                       .then_inc(reset_done, 1)
                    dve.wait_ge(lif_xt_done, m + 1)
                    wait(dve, stored[t % 4], y * 32 + (t // 4) * 16)
                    dve.scalar_tensor_tensor(xstage[:, t % 4, :], charged[t % 2][:, :], 1.0, banks[2 + t % 2], ALU.is_ge, ALU.add)\
                       .then_inc(spike_done, 1)

            lif_units(0)
            with dve.Fori(1, WROWS) as y:
                lif_units(y)

        @block.tensor
        def _(pe):
            pe.wait_ge(const_step, 4)
            pe.wait_ge(w_loaded, 32)
            for b in range(4):
                for j in range(4):
                    tile = (b % 2) * 4 + j
                    last = pe.transpose(banks[b][:, j * 128:(j + 1) * 128],
                                        wstage[:, tile, (b // 2) * 128:(b // 2 + 1) * 128], ident[:, :])
                last.then_inc(setup_pe, 1)
            pe.wait_ge(tab_loaded, 16 * 2 * WIN)
            for j in range(2):
                last = pe.matmul(pv_ps[:, j, :], flip[:, :], bias_raw[:, j * 512:(j + 1) * 512], start=True, stop=True)
            last.then_inc(setup_pe, 1)
            pe.wait_ge(setup_dve, 4)
            for v in range(4):
                for j in range(4):
                    last = pe.transpose(banks[4 + v][:, j * 128:(j + 1) * 128], bias_sum[:, v, j * 128:(j + 1) * 128],
                                        ident[:, :])
                last.then_inc(setup_pe, 1)
            pe.wait_ge(setup_dve, 5)

            def turn_sample(s):
                for slot in range(4):
                    pe.wait_ge(in_loaded[slot], (s + 1) * 16)
                    wait(pe, in_kept[slot], s)
                    for h in range(HALVES):
                        for a in range(2):
                            last = pe.transpose(banks[slot][:, h * ROWTOK + a * 128:h * ROWTOK + (a + 1) * 128],
                                                xstage[:, slot, a * C + h * 128:a * C + (h + 1) * 128], ident[:, :])
                    last.then_inc(in_turned[slot], 1)

            turn_sample(0)
            with pe.Fori(1, SAMPLES) as s:
                turn_sample(s)

            def group_averages(layer):
                first = (layer - 1) * NORM_STEPS
                pe.wait_ge(const_step, 6)
                pe.wait_ge(norm_dve, first + 1)
                pe.matmul(proj_ps[:, 0, 0:NORMS], group_avg[:, :], moments[:, :, 0], start=True, stop=True).then_inc(norm_pe, 1)
                pe.wait_ge(norm_dve, first + 4)
                pe.matmul(proj_ps[:, 0, NORMS:2 * NORMS], group_avg[:, :], tiny[2][:, :], start=True, stop=True).then_inc(norm_pe, 1)

            pe.wait_ge(setup_act, SETUP_ACT)
            group_averages(1)

            def project_channels(bank, first, slot):
                for h in range(HALVES):
                    dst = proj_ps[:, bank, h * ROWTOK:(h + 1) * ROWTOK]
                    cols = slice(first + h * 128, first + (h + 1) * 128)
                    pe.matmul(dst, b_row[:, cols], ones_r[:, :], start=True, stop=False)
                    for c in range(HALVES):
                        tok = slice(c * ROWTOK, (c + 1) * ROWTOK)
                        pe.matmul(dst, w_hi[:, c, cols], xn_hi[slot][:, tok], start=False, stop=False)
                        pe.matmul(dst, w_hi[:, c, cols], xn_lo[slot][:, tok], start=False, stop=False)
                        last = pe.matmul(dst, w_lo[:, c, cols], xn_hi[slot][:, tok], start=False, stop=(c == HALVES - 1))
                return last

            def project_tokens(dst, tile, first, slot, bias):
                cols = slice(first, first + C)
                if bias:
                    pe.matmul(dst, ones_r[:, 0:128], b_row[:, cols], start=True, stop=False)
                for c in range(HALVES):
                    tok = slice(c * ROWTOK + tile * 128, c * ROWTOK + (tile + 1) * 128)
                    pe.matmul(dst, xn_hi[slot][:, tok], w_hi[:, c, cols], start=(c == 0 and not bias), stop=False)
                    pe.matmul(dst, xn_hi[slot][:, tok], w_lo[:, c, cols], start=False, stop=False)
                    last = pe.matmul(dst, xn_lo[slot][:, tok], w_hi[:, c, cols], start=False, stop=(c == HALVES - 1))
                return last

            def project_q(slot, r):
                pe.wait_ge(xn_lo_done, r + 1)
                wait(pe, v_lo_done, r)
                project_channels(0, 0, slot).then_inc(q_ps_done, 1)

            def project_k(slot, r):
                wait(pe, x1_kept, 2 * r - 4)
                project_channels(1, C, slot).then_inc(k_ps_done, 1)

            def project_v(slot, r):
                pe.wait_ge(q_lo_done, r + 1)
                for p in range(2):
                    last = project_tokens(proj_ps[:, 0, p * C:(p + 1) * C], p, 2 * C, slot, False)
                last.then_inc(v_ps_done, 1)

            def variant(row, k, w):
                wx = 2 * (k % 2) + w
                at_x = 1 if wx == WCOLS - 1 else 0
                if isinstance(row, int):
                    return 2 * (row % WROWS == WROWS - 1) + at_x
                if k // 2 == 0:
                    return at_x
                return ((row >> 1) & 1) * 2 + at_x

            def table(tensor, v):
                if isinstance(v, int):
                    return tensor[:, v, :]
                return tensor[:, bass.ds(v, 1), :].rearrange("p a n -> p (a n)")

            def max_scores(m, row, k):
                slot = k // 2
                pe.wait_ge(k_hi_done, row + 1)
                wait(pe, max_rows_done, m)
                for w in range(2):
                    pe.matmul(max_ps[:, w, :], ident_r[:, :], table(bias_q, variant(row, k, w)), start=True, stop=False)
                    wx = 2 * (k % 2) + w
                    for h in range(HALVES):
                        for mid in range(2):
                            at = (2 * h + mid) * 128
                            last = pe.matmul(max_ps[:, w, at:at + 128],
                                             q_hi[slot][:, h, wx, 2 * mid:2 * mid + 2, :].rearrange("p q i -> p (q i)"),
                                             k_hi[slot][:, h, wx, :, :].rearrange("p e j -> p (e j)"),
                                             start=False, stop=(h == 1 and mid == 1))
                last.then_inc(max_ps_done, 1)

            def scores(n, row, k):
                slot, p = k // 2, k % 2
                pe.wait_ge(k_lo_done, row + 1)
                for w in range(2):
                    wx = 2 * p + w
                    wait(pe, p_hi_done, n * 2 + (w - 1))
                    v = variant(row, k, w)
                    pe.matmul(score_ps[:, w, :], ident_r[:, :], table(bias_hi, v), start=True, stop=False)
                    pe.matmul(score_ps[:, w, :], ident_r[:, :], table(bias_lo, v), start=False, stop=False)
                    for h in range(HALVES):
                        dst = score_ps[:, w, h * 256:(h + 1) * 256]
                        for kk, qq in ((k_hi, q_hi), (k_hi, q_lo), (k_lo, q_hi)):
                            pe.matmul(dst, kk[slot][:, h, wx, :, :].rearrange("p e j -> p (e j)"),
                                      qq[slot][:, h, wx, :, :].rearrange("p q i -> p (q i)"), start=False, stop=False)
                pe.wait_ge(max_rows_done, n + 1)
                for w in range(2):
                    for b in range(4):
                        last = pe.matmul(score_ps[:, w, b * 128:(b + 1) * 128], pick_max[:, 4 * w + b, :], max_rows[p][:, :],
                                         start=False, stop=(b == 3))
                    last.then_inc(score_ps_done, 1)

            def turn_maxima(n, p):
                pe.wait_ge(max_split_done, n + 1)
                pe.transpose(max_ps[:, 0, :].bitcast(bf16)[0:32, 0:128], max_split[p][:, :], ident_b[:, :])\
                  .then_inc(max_turned, 1)

            def weigh_values(m, row, k):
                p = k % 2
                pe.wait_ge(p_lo_done, m * 2 + 2)
                pe.wait_ge(v_lo_done, row + 1)
                wait(pe, attn_done, m)
                for h in range(HALVES):
                    cols = pv_ps[:, h, 0:2 * WIN_N].rearrange("p (w g n) -> p w g n", w=2, g=QUADS)
                    for g in range(QUADS):
                        for at, (pp, vv) in enumerate(((p_hi, v_hi), (p_hi, v_lo), (p_lo, v_hi))):
                            last = pe.matmul(cols[:, :, g, :], pp[p][:, h * QUADS + g, :, :].rearrange("p w i -> p (w i)"),
                                             vv[k][:, h, :, g, :, :].rearrange("p w e d -> p w (e d)"),
                                             start=(at == 0), stop=(at == 2))
                last.then_inc(pv_ps_done, 1)

            def turn_x1(m, k):
                pe.wait_ge(x1_done, m + 1)
                wait(pe, x1_kept, m)
                for h in range(HALVES):
                    last = pe.transpose(proj_ps[:, 1, h * 128:(h + 1) * 128], x1[k % 2][:, h * 128:(h + 1) * 128],
                                        ident[:, :])
                last.then_inc(x1_turned, 1)

            pe.wait_ge(setup_dve, SETUP_DVE)
            project_q(0, 0)
            project_k(0, 0)
            project_v(0, 0)
            max_scores(0, 0, 0)

            def pair(n, row, k):
                p = k % 2
                nxt = 1 - k // 2
                if not is_last_row(row):
                    if p == 0:
                        project_q(nxt, row + 1)
                        project_k(nxt, row + 1)
                    else:
                        project_v(nxt, row + 1)
                turn_maxima(n, p)
                scores(n, row, k)
                if not is_first(n, 1):
                    weigh_values(n - 1, row if p else row - 1, (k - 1) % 4)
                if not is_first(n, 2):
                    if p == 0 and not is_last_row(row):
                        pe.wait_ge(k_lo_done, row + 2)
                    turn_x1(n - 2, k)
                if not (isinstance(n, int) and n + 1 >= PAIRS):
                    max_scores(n + 1, row + 1 if p else row, (k + 1) % 4)

            run(pe, pair)
            weigh_values(PAIRS - 1, ROWS - 1, 3)
            turn_x1(PAIRS - 2, 0)
            turn_x1(PAIRS - 1, 1)
            pe.wait_ge(x1_kept, PAIRS)
            group_averages(2)
            pe.wait_ge(norm_ready, 2)

            def lif_units(y):
                for t in range(SAMPLES):
                    m = y * SAMPLES + t
                    s = t % 2
                    pe.wait_ge(lif_loaded[s], y * 64 + (t // 2 + 1) * 16)
                    wait(pe, spike_done, y * SAMPLES + (t - 1))
                    for h in range(HALVES):
                        for a in range(2):
                            last = pe.transpose(banks[2 + s][:, a * C + h * 128:a * C + (h + 1) * 128],
                                                lif_x[s][:, h * ROWTOK + a * 128:h * ROWTOK + (a + 1) * 128], ident[:, :])
                    last.then_inc(lif_xt_done, 1)
                    pe.wait_ge(xn_lo_done, y * SAMPLES + (ROWS + t + 1))
                    for a in range(2):
                        last = project_tokens(banks[s][:, a * C:(a + 1) * C], a, 3 * C, s, True)
                    last.then_inc(h_ps_done, 1)

            lif_units(0)
            with pe.Fori(1, WROWS) as y:
                lif_units(y)


_INS = ['x', 'L0_conv_qkv_w', 'L0_conv_qkv_b', 'L0_conv_bias_table', 'L1_conv_W', 'L1_conv_b']


def kernel(**inputs):
    import numpy as _np
    import concourse.bacc as _bacc
    from concourse import mybir as _mybir
    from concourse.bass_utils import run_bass_kernel_spmd as _run

    nc = _bacc.Bacc("TRN2", target_bir_lowering=False, num_devices=1)
    arrays, args = {}, []
    for name in _INS:
        a = _np.ascontiguousarray(inputs[name])
        arrays[f"in_{name}_dram"] = a
        args.append(nc.dram_tensor(f"in_{name}_dram", a.shape, _mybir.dt.from_np(a.dtype), kind="ExternalInput").ap())
    shape = arrays["in_x_dram"].shape
    args.append(nc.dram_tensor("out_0_dram", shape, _mybir.dt.float32, kind="ExternalOutput").ap())
    swin_attention_then_lif_kernel(nc, *args)
    r = _run(nc, [arrays], core_ids=[0])
    return r.results[0]["out_0_dram"]
```

```python
import concourse.bass as bass
from concourse import mybir
from contextlib import ExitStack


def swin_attention_then_lif_kernel(nc, x, qkv_w, qkv_b, bias_table, lif_w, lif_b, out):
    f32, f32r = mybir.dt.float32, mybir.dt.float32r
    f16, bf16, i32 = mybir.dt.float16, mybir.dt.bfloat16, mybir.dt.int32
    ALU = mybir.AluOpType
    ACT = mybir.ActivationFunctionType
    AX = mybir.AxisListType

    SAMPLES, HEIGHT, WIDTH, C = x.shape
    WIN = 8
    WS = WIN * WIN
    HEADS = bias_table.shape[1]
    D = C // HEADS
    HALVES = C // 128
    WROWS = HEIGHT // WIN
    WCOLS = WIDTH // WIN
    ROWS = SAMPLES * WROWS
    PAIRS = ROWS * 2
    ROWTOK = WCOLS * WS
    QUADS = 4
    QK_SCALE = float(D) ** -0.5
    TAU = 2.0
    EPS = 1e-5
    GROUP = C // 32
    MASK = -100.0
    OUTS = 3 * C + C
    PV_N = 2 * (D + 1)
    WIN_N = QUADS * PV_N

    x_windows = x.rearrange("s (y yi) (wx xi) c -> (s y) wx yi xi c", yi=WIN, xi=WIN)
    x_rows = x.rearrange("s (y a yi) w c -> (s y) (yi w) a c", a=2, yi=WIN // 2)
    out_rows = out.rearrange("s (y a yi) w c -> (s y) (yi w) a c", a=2, yi=WIN // 2)

    ctx = ExitStack()
    with ctx:
        def sb(name, shape, dt):
            return ctx.enter_context(nc.sbuf_tensor(name, shape, dt))

        def sem(name):
            return ctx.enter_context(nc.semaphore(name))

        xc = sb("xc", [128, ROWS, HALVES * ROWTOK], f32)
        w_hi = sb("w_hi", [128, HALVES, OUTS], f32r)
        w_lo = sb("w_lo", [128, HALVES, OUTS], f32r)
        b_row = sb("b_row", [128, OUTS], f32r)
        ones_r = sb("ones_r", [128, ROWTOK], f32r)
        vbias = sb("vbias", [128, C], f32)
        ident = sb("ident", [128, 128], f32)
        ident_r = sb("ident_r", [128, 128], f32r)
        ident_b = sb("ident_b", [128, 128], bf16)
        group_avg = sb("group_avg", [128, 128], f32)
        parity_mask = sb("parity_mask", [128, 2], f32)
        pick_max = sb("pick_max", [128, 2 * QUADS, 128], bf16)
        bias_hi = sb("bias_hi", [128, 4, 512], f32r)
        bias_lo = sb("bias_lo", [128, 4, 512], f32r)
        bias_q = sb("bias_q", [128, 4, 512], f32r)
        stats = sb("stats", [128, ROWS, HALVES, 6], f32)
        moments = sb("moments", [128, SAMPLES * HALVES, 2], f32)
        neg_mean = sb("neg_mean", [128, (SAMPLES + 1) * HALVES], f32)
        rstd = sb("rstd", [128, (SAMPLES + 1) * HALVES], f32)
        shift = sb("shift", [128, (SAMPLES + 1) * HALVES], f32)
        tiny = [sb(f"tiny{i}", [128, SAMPLES * HALVES], f32) for i in range(6)]

        wstage = sb("wstage", [128, OUTS // 128, C], f32)
        bias_sum = wstage[:, :, :].rearrange("p t c -> p (t c)").rearrange("p (v n) -> p v n", v=4)
        bias_raw = sb("bias_raw", [128, WIN * WIN * HEADS], f32)
        flip = sb("flip", [128, 128], f32)
        masks = sb("masks", [128, 4, WS], f32)
        bits = sb("bits", [128, 4], i32)
        flags = sb("flags", [128, 3], f32)
        xstage = sb("xstage", [128, 4, 2 * C], f32)
        xn = [sb(f"xn{i}", [128, HALVES * ROWTOK], f32) for i in range(2)]
        xn_hi = [sb(f"xn_hi{i}", [128, HALVES * ROWTOK], f32r) for i in range(2)]
        xn_lo = [sb(f"xn_lo{i}", [128, HALVES * ROWTOK], f32r) for i in range(2)]
        q_flat = sb("q_flat", [128, 2, HALVES * ROWTOK], f16)
        q_hi = [sb(f"q_hi{i}", [128, HALVES, WCOLS, QUADS, WS], f16) for i in range(2)]
        q_lo = [sb(f"q_lo{i}", [128, QUADS, HALVES * ROWTOK], f16) for i in range(2)]
        k_hi = [sb(f"k_hi{i}", [128, HALVES, WCOLS, 2, WS], f16) for i in range(2)]
        k_lo = [sb(f"k_lo{i}", [128, HALVES, WCOLS, 2, WS], f16) for i in range(2)]
        v_hi = [sb(f"v_hi{i}", [128, HALVES, 2, QUADS, 2, D + 1], f16) for i in range(4)]
        v_lo = [sb(f"v_lo{i}", [128, HALVES, 2, QUADS, 2, D + 1], f16) for i in range(4)]
        probs = sb("probs", [128, 2 * QUADS, 2, WS], f32)
        p_hi = [sb(f"p_hi{i}", [128, 2 * QUADS, 2, WS], f16) for i in range(2)]
        p_lo = [sb(f"p_lo{i}", [128, 2 * QUADS, 2, WS], f16) for i in range(2)]
        neg_max = sb("neg_max", [128, 16], f32)
        max_split = [sb(f"max_split{i}", [128, 32], bf16) for i in range(2)]
        max_rows = [sb(f"max_rows{i}", [128, 128], bf16) for i in range(2)]
        b_raw = probs[:, :, :, :].rearrange("p g w i -> p (g w i)")
        recip = sb("recip", [128, HALVES, 2, 2 * QUADS], f32)
        attn = [sb(f"attn{i}", [128, HALVES, 2 * QUADS, D], f32) for i in range(2)]
        x1 = [sb(f"x1_{i}", [128, C], f32) for i in range(2)]
        lif_x = [q[:, :, :].bitcast(f32).rearrange("p g n -> p (g n)")[:, i * 512:(i + 1) * 512]
                 for q in q_lo for i in range(2)]
        charged = [q[:, :, :, :, :].bitcast(f32).rearrange("p h w g i -> p (h w g i)")[:, 0:2 * C]
                   for q in q_hi]
        membrane = k_hi[0][:, :, :, :, :].bitcast(f32).rearrange("p h w e j -> p (h w e j)")

        max_ps, score_ps, pv_ps, proj_ps = [
            ctx.enter_context(nc.psum_tensor(name, [128, 2, 512], f32))
            for name in ("max_ps", "score_ps", "pv_ps", "proj_ps")]
        banks = [t[:, j, :] for t in (max_ps, score_ps, pv_ps, proj_ps) for j in range(2)]

        w_loaded = sem("w_loaded")
        tab_loaded = sem("tab_loaded")
        b_loaded = sem("b_loaded")
        vb_loaded = sem("vb_loaded")
        const_step = sem("const_step")
        setup_pe = sem("setup_pe")
        setup_act = sem("setup_act")
        setup_dve = sem("setup_dve")
        mask_step = sem("mask_step")
        in_loaded = [sem(f"in_loaded{i}") for i in range(4)]
        in_turned = [sem(f"in_turned{i}") for i in range(4)]
        in_kept = [sem(f"in_kept{i}") for i in range(4)]
        stats_done = sem("stats_done")
        norm_pe = sem("norm_pe")
        norm_act = sem("norm_act")
        norm_dve = sem("norm_dve")
        norm_ready = sem("norm_ready")
        xn_done = sem("xn_done")
        xn_hi_done = sem("xn_hi_done")
        xn_lo_done = sem("xn_lo_done")
        q_ps_done = sem("q_ps_done")
        k_ps_done = sem("k_ps_done")
        v_ps_done = sem("v_ps_done")
        q_flat_done = sem("q_flat_done")
        q_hi_done = sem("q_hi_done")
        k_hi_done = sem("k_hi_done")
        v_hi_done = sem("v_hi_done")
        q_lo_done = sem("q_lo_done")
        q_spread = [sem(f"q_spread{i}") for i in range(2)]
        k_lo_done = sem("k_lo_done")
        v_lo_done = sem("v_lo_done")
        max_ps_done = sem("max_ps_done")
        neg_max_done = sem("neg_max_done")
        max_hi_done = sem("max_hi_done")
        max_split_done = sem("max_split_done")
        max_turned = sem("max_turned")
        max_rows_done = sem("max_rows_done")
        score_ps_done = sem("score_ps_done")
        p_hi_done = sem("p_hi_done")
        p_lo_done = sem("p_lo_done")
        pv_ps_done = sem("pv_ps_done")
        recip_done = sem("recip_done")
        attn_done = sem("attn_done")
        res_loaded = [sem(f"res_loaded{i}") for i in range(4)]
        res_done = sem("res_done")
        x1_done = sem("x1_done")
        x1_turned = sem("x1_turned")
        x1_kept = sem("x1_kept")
        lif_loaded = [sem(f"lif_loaded{i}") for i in range(4)]
        h_ps_done = sem("h_ps_done")
        lif_xt_done = sem("lif_xt_done")
        charge_done = sem("charge_done")
        reset_done = sem("reset_done")
        spike_done = sem("spike_done")
        stored = [sem(f"stored{i}") for i in range(4)]

        def wait(eng, s, value):
            if not isinstance(value, int) or value > 0:
                eng.wait_ge(s, value)

        def one(tensor, row):
            return tensor[:, bass.ds(row, 1), :].rearrange("p a n -> p (a n)")

        def sample_of(row):
            return row // WROWS if isinstance(row, int) else row >> (WROWS.bit_length() - 1)

        def run(eng, body):
            for k in range(BODY):
                body(k, k // 2, k)
            with eng.Fori(1, LAST) as i:
                for k in range(BODY):
                    body(i * BODY + k, i * 2 + k // 2, k)
            for k in range(BODY):
                body(LAST * BODY + k, LAST * 2 + k // 2, k)

        def spread_of_row(n, k):
            return (n + (BODY - k)) * 16

        def is_first(n, lag):
            return isinstance(n, int) and n < lag

        def is_last_row(row, ahead=1):
            return isinstance(row, int) and row + ahead >= ROWS

        def is_last_y(y):
            return isinstance(y, int) and y == WROWS - 1

        def over_y(eng, body):
            body(0)
            with eng.Fori(1, WROWS - 1) as y:
                body(y)
            body(WROWS - 1)

        AHEAD = 3
        BODY = 4
        LAST = PAIRS // BODY - 1
        W_TILES = OUTS // 128
        W_SCALES = [QK_SCALE, 1.0, 1.0, 1.0 / TAU]

        NORMS = SAMPLES * HALVES
        NORM_STEPS = 10
        SETUP_DVE = 6
        SETUP_ACT = 14

        def v_part(p, w, e):
            return proj_ps[w * WS:(w + 1) * WS, 0, p * C:(p + 1) * C]\
                .rearrange("p (h g e d) -> p h g e d", h=HALVES, g=QUADS, e=2)[:, :, :, e, :]

        block = ctx.enter_context(nc.Block())

        @block.sync
        def _(sp):
            sp.dma_start(wstage[:, 0:3 * C // 128, :], qkv_w.rearrange("(t p) c -> p t c", p=128)).then_inc(w_loaded, 16)
            sp.dma_start(wstage[:, 3 * C // 128:W_TILES, :], lif_w.rearrange("(t p) c -> p t c", p=128)).then_inc(w_loaded, 16)
            def load_sample(s):
                for slot in range(4):
                    wait(sp, in_turned[slot], s)
                    sp.dma_start(xstage[:, slot, :].rearrange("p (a c) -> p a c", a=2),
                                 x_rows[bass.ds(s * WROWS + slot, 1)].rearrange("r p a c -> p (r a) c"))\
                      .then_inc(in_loaded[slot], 16)

            load_sample(0)
            with sp.Fori(1, SAMPLES) as s:
                load_sample(s)

            def load_residual(row, p, slot):
                for w in range(2):
                    sp.dma_start(xstage[w * WS:(w + 1) * WS, slot, 0:C],
                                 x_windows[bass.ds(row, 1), 2 * p + w]).then_inc(res_loaded[slot], 16)

            def spread_q(slot, done):
                sp.wait_ge(q_lo_done, done)
                for g in range(QUADS):
                    rows = slice(32 * g, 32 * g + 32)
                    sp.dma_start(q_lo[slot][rows, g, :], q_flat[rows, 1, :]).then_inc(q_spread[slot], 16)

            for slot in range(4):
                sp.wait_ge(in_turned[slot], SAMPLES)
                load_residual(slot // 2, slot % 2, slot)
            sp.wait_ge(const_step, 8)
            spread_q(0, 1)

            def pair(n, row, k):
                if k % 2 == 0 and not is_last_row(row):
                    spread_q(1 - k // 2, row + 2)
                if not is_first(n, 1) and not (isinstance(n, int) and n + 3 >= PAIRS):
                    sp.wait_ge(x1_done, n)
                    load_residual(row + (1 + k % 2), (k + 3) % 2, (k + 3) % 4)

            run(sp, pair)

            sp.wait_ge(norm_ready, 2)

            def store(y, t):
                slot = t % 4
                sp.wait_ge(spike_done, y * SAMPLES + (t + 1))
                sp.dma_start(out_rows[bass.ds(y + t * WROWS, 1)].rearrange("r p a c -> p (r a) c"),
                             xstage[:, slot, :].rearrange("p (a c) -> p a c", a=2)).then_inc(stored[slot], 16)

            def load(y, t):
                wait(sp, lif_xt_done, y * SAMPLES + (t - 3))
                sp.dma_start(lif_x[t % 4], one(xc, y + t * WROWS)).then_inc(lif_loaded[t % 4], 16)

            def lif_units(y):
                for t in range(SAMPLES):
                    if t + AHEAD < SAMPLES:
                        load(y, t + AHEAD)
                    elif not is_last_y(y):
                        load(y + 1, t + AHEAD - SAMPLES)
                    store(y, t)

            for t in range(AHEAD):
                load(0, t)
            over_y(sp, lif_units)
            for slot in range(4):
                sp.wait_ge(stored[slot], 16 * SAMPLES * WROWS // 4)

        @block.gpsimd
        def _(pool):
            pool.memset(ident[:, :], 0.0).then_inc(const_step, 1)
            pool.memset(flip[:, :], 0.0)
            pool.memset(group_avg[:, :], 1.0 / GROUP).then_inc(const_step, 1)
            pool.iota(bits[:, 0:1], pattern=[[0, 1]], base=0, channel_multiplier=1).then_inc(const_step, 1)
            pool.wait_ge(const_step, 3)
            pool.affine_select(out=ident[:, :], in_=ident[:, :], compare_op=ALU.not_equal, fill=1.0, base=0,
                               pattern=[[-1, 128]], channel_multiplier=1)
            pool.affine_select(out=flip[:, :], in_=flip[:, :], compare_op=ALU.not_equal, fill=1.0, base=-127,
                               pattern=[[1, 128]], channel_multiplier=1).then_inc(const_step, 1)
            grp = group_avg[:, :].rearrange("p (g e) -> p g e", e=GROUP)
            pool.affine_select(out=grp, in_=grp, compare_op=ALU.is_ge, fill=0.0, base=0,
                               pattern=[[-GROUP, 128 // GROUP], [0, GROUP]], channel_multiplier=1).then_inc(const_step, 1)
            pool.wait_ge(const_step, 5)
            pool.affine_select(out=grp, in_=grp, compare_op=ALU.is_ge, fill=0.0, base=GROUP - 1,
                               pattern=[[GROUP, 128 // GROUP], [0, GROUP]], channel_multiplier=-1).then_inc(const_step, 1)
            for buf in q_lo:
                pool.memset(buf[:, :, :], 0.0)
            for buf in q_hi + k_hi + k_lo:
                pool.memset(buf[:, :, :, :, :], 0.0)
            for buf in v_hi + v_lo:
                pool.memset(buf[:, :, :, :, :, :], 0.0)
            for buf in max_rows:
                zeroed = pool.memset(buf[:, :], 0.0)
            zeroed.then_inc(const_step, 1)
            pool.wait_ge(const_step, 7)
            for buf in v_hi:
                for e in range(2):
                    for h in range(HALVES):
                        ones = pool.memset(buf[e * WS:(e + 1) * WS, h, :, :, e, D:D + 1], 1.0)
            ones.then_inc(const_step, 1)
            pool.wait_ge(const_step, 8)

            def low_part(slot, done):
                pool.wait_ge(xn_hi_done, done)
                pool.tensor_tensor(xn_lo[slot][:, :], xn[slot][:, :], xn_hi[slot][:, :].bitcast(f32), ALU.subtract)\
                    .then_inc(xn_lo_done, 1)

            for r in range(2):
                low_part(r, r + 1)
            pool.wait_ge(vb_loaded, 16)

            def add_residual(m, k):
                pool.wait_ge(attn_done, m + 1)
                pool.wait_ge(res_done, m + 1)
                wait(pool, x1_turned, m - 1)
                pool.tensor_tensor(x1[k % 2][:, :], attn[k % 2][:, :, :, :].rearrange("p h n d -> p (h n d)"),
                                   xstage[:, k, 0:C], ALU.add).then_inc(x1_done, 1)

            def pair(n, row, k):
                p = k % 2
                if p == 1 and not is_last_row(row, 2):
                    low_part(k // 2, row + 3)
                pool.wait_ge(res_loaded[k], (n // 4 + 1) * 32 if isinstance(n, int) else (n + (BODY - k)) * (32 // BODY))
                pool.tensor_tensor(xstage[:, k, 0:C], xstage[:, k, 0:C], vbias[:, :], ALU.add).then_inc(res_done, 1)
                wait(pool, pv_ps_done, n - 1)
                for w in range(2):
                    pool.wait_ge(p_hi_done, n * 2 + (w + 1))
                    pool.tensor_tensor(p_lo[p][:, :, w, :], probs[:, :, w, :], p_hi[p][:, :, w, :], ALU.subtract)\
                        .then_inc(p_lo_done, 1)

                if not is_first(n, 1):
                    add_residual(n - 1, (k - 1) % 4)

            run(pool, pair)
            add_residual(PAIRS - 1, 3)

            def lif_units(y):
                for t in range(SAMPLES):
                    low_part(t % 2, y * SAMPLES + (ROWS + t + 1))

            over_y(pool, lif_units)

        @block.scalar
        def _(act):
            span = 2 * WIN - 1
            for e in range(2):
                for yj in range(WIN):
                    src = bass.AP(tensor=bias_table.tensor, offset=yj * span * HEADS,
                                  ap=[[HEADS, WIN], [span * HEADS, WIN], [1, WIN * HEADS]])
                    act.dma_start(bias_raw[e * WS + yj * WIN:e * WS + (yj + 1) * WIN, :], src).then_inc(tab_loaded, 16)
            act.dma_start(vbias[:, :], qkv_b[2 * C:3 * C].partition_broadcast(128)).then_inc(vb_loaded, 16)
            act.wait_ge(setup_dve, 1)
            for r in (0, 32):
                act.dma_start(b_raw[r:r + 1, 0:3 * C], qkv_b.rearrange("(o c) -> o c", o=1)).then_inc(b_loaded, 16)
                act.dma_start(b_raw[r:r + 1, 3 * C:OUTS], lif_b.rearrange("(o c) -> o c", o=1)).then_inc(b_loaded, 16)
            for b in range(4):
                act.wait_ge(setup_pe, b + 1)
                for j in range(2):
                    kind = (b % 2) * 2 + j
                    act.activation(w_hi[:, b // 2, kind * C:(kind + 1) * C], banks[b][:, j * C:(j + 1) * C], ACT.Copy,
                                   scale=W_SCALES[kind]).then_inc(setup_act, 1)
            act.wait_ge(setup_dve, 3)
            act.activation(b_row[:, :], b_raw, ACT.Copy).then_inc(setup_act, 1)
            act.wait_ge(setup_dve, 4)
            act.activation(bias_hi[:, :, :], bias_sum, ACT.Copy).then_inc(setup_act, 1)
            for v in range(4):
                act.wait_ge(setup_pe, 6 + v)
                act.activation(bias_q[:, v, :], banks[4 + v], ACT.Copy).then_inc(setup_act, 1)

            with act.Fori(0, SAMPLES) as s:
                for slot in range(4):
                    act.wait_ge(in_turned[slot], s + 1)
                    for h in range(HALVES):
                        src = banks[slot][:, h * ROWTOK:(h + 1) * ROWTOK].rearrange("p (y w x) -> p w y x", y=WIN, w=WCOLS)
                        dst = one(xc, s * WROWS + slot)[:, h * ROWTOK:(h + 1) * ROWTOK]\
                            .rearrange("p (w y x) -> p w y x", y=WIN, w=WCOLS)
                        last = act.activation(dst, src, ACT.Copy)
                    last.then_inc(in_kept[slot], 1)

            def square_root(done):
                act.wait_ge(norm_dve, done)
                act.activation(tiny[5][:, :], tiny[4][:, :], ACT.Sqrt).then_inc(norm_act, 1)

            def normalise(row, sample, slot, layer, done):
                act.wait_ge(norm_ready, layer)
                wait(act, xn_lo_done, done - 1)
                for h in range(HALVES):
                    col = bass.ds(sample * HALVES + h, 1)
                    last = act.activation(xn[slot][:, h * ROWTOK:(h + 1) * ROWTOK],
                                          one(xc, row)[:, h * ROWTOK:(h + 1) * ROWTOK], ACT.Identity,
                                          bias=shift[:, col], scale=rstd[:, col])
                last.then_inc(xn_done, 1)

            def xn_high(slot, done):
                act.wait_ge(xn_done, done)
                act.activation(xn_hi[slot][:, :], xn[slot][:, :], ACT.Copy).then_inc(xn_hi_done, 1)

            def q_high(done):
                act.wait_ge(q_ps_done, done)
                wait(act, q_hi_done, done - 1)
                act.activation(q_flat[:, 0, :], proj_ps[:, 0, :], ACT.Copy).then_inc(q_flat_done, 1)

            def k_high(slot, done):
                act.wait_ge(k_ps_done, done)
                for e in range(2):
                    last = act.activation(k_hi[slot][:, :, :, e, :].rearrange("p h w j -> p (h w) j"),
                                          proj_ps[:, 1, :].rearrange("p (n j) -> p n j", j=WS), ACT.Copy,
                                          scale=parity_mask[:, e:e + 1])
                last.then_inc(k_hi_done, 1)

            def v_high(slot, done):
                act.wait_ge(v_ps_done, done)
                for p in range(2):
                    for w in range(2):
                        for e in range(2):
                            last = act.activation(v_hi[2 * slot + p][e * WS:(e + 1) * WS, :, w, :, e, 0:D],
                                                  v_part(p, w, e), ACT.Copy)
                last.then_inc(v_hi_done, 1)

            square_root(NORM_STEPS - 5)
            normalise(0, 0, 0, 1, 0)
            normalise(1, 0, 1, 1, 1)
            xn_high(0, 1)
            act.wait_ge(setup_dve, SETUP_DVE)
            act.wait_ge(const_step, 8)
            q_high(1)
            k_high(0, 1)
            v_high(0, 1)
            xn_high(1, 2)

            def keep_x1(m, row, k):
                act.wait_ge(x1_turned, m + 1)
                for h in range(HALVES):
                    src = proj_ps[:, 1, h * 128:(h + 1) * 128].rearrange("p (w y x) -> p w y x", w=2, y=WIN)
                    dst = one(xc, row)[:, h * ROWTOK:(h + 1) * ROWTOK]\
                        .rearrange("p (y w x) -> p w y x", y=WIN, w=WCOLS)[:, 2 * (k % 2):2 * (k % 2) + 2]
                    last = act.activation(dst, src, ACT.Copy)
                last.then_inc(x1_kept, 1)

            def pair(n, row, k):
                p = k % 2
                nxt = 1 - k // 2
                if not is_last_row(row):
                    if p == 0:
                        q_high(row + 2)
                        k_high(nxt, row + 2)
                    else:
                        v_high(nxt, row + 2)
                if p == 1 and not is_last_row(row, 2):
                    xn_high(k // 2, row + 3)
                act.wait_ge(max_turned, n + 1)
                act.activation(max_rows[p][0:32, :], max_ps[:, 0, :].bitcast(bf16)[0:32, 0:128], ACT.Copy)\
                    .then_inc(max_rows_done, 1)
                if p == 0 and not is_last_row(row, 2):
                    normalise(row + 2, sample_of(row + 2), k // 2, 1, row + 2)
                wait(act, pv_ps_done, n - 1)
                for w in range(2):
                    wait(act, p_lo_done, n * 2 + (w - 1))
                    act.wait_ge(score_ps_done, n * 2 + (w + 1))
                    scores = score_ps[:, w, :].rearrange("p (g i) -> p g i", i=WS)
                    act.activation(probs[:, :, w, :], scores, ACT.Exp)
                    act.activation(p_hi[p][:, :, w, :], scores, ACT.Exp).then_inc(p_hi_done, 1)
                if not is_first(n, 2):
                    keep_x1(n - 2, row - 1, k)

            run(act, pair)
            keep_x1(PAIRS - 2, ROWS - 1, 0)
            keep_x1(PAIRS - 1, ROWS - 1, 1)
            square_root(2 * NORM_STEPS - 5)
            normalise(0, 0, 0, 2, ROWS)

            def lif_units(y):
                for t in range(SAMPLES):
                    m = y * SAMPLES + t
                    wait(act, h_ps_done, m - 1)
                    xn_high(t % 2, y * SAMPLES + (ROWS + t + 1))
                    if t + 1 < SAMPLES:
                        normalise(y + (t + 1) * WROWS, t + 1, (t + 1) % 2, 2, m + (ROWS + 1))
                    elif not is_last_y(y):
                        normalise(y + 1, 0, 0, 2, m + (ROWS + 1))

            over_y(act, lif_units)

        @block.vector
        def _(dve):
            dve.memset(b_raw, 0.0).then_inc(setup_dve, 1)
            dve.memset(ones_r[:, :].bitcast(f32), 1.0)
            dve.memset(masks[:, :, :], 0.0).then_inc(setup_dve, 1)
            dve.wait_ge(b_loaded, 64)
            for r in (0, 32):
                dve.tensor_scalar(b_raw[r:r + 1, 0:C], b_raw[r:r + 1, 0:C], QK_SCALE, None, ALU.mult)
                last = dve.tensor_scalar(b_raw[r:r + 1, 3 * C:OUTS], b_raw[r:r + 1, 3 * C:OUTS], 1.0 / TAU, None, ALU.mult)
            last.then_inc(setup_dve, 1)
            dve.wait_ge(const_step, 4)
            for j, bit in enumerate((4, 32, 16)):
                last = dve.tensor_scalar(bits[:, j + 1:j + 2], bits[:, 0:1], bit, None, ALU.bitwise_and)
            last.then_inc(mask_step, 1)
            dve.wait_ge(setup_dve, 2)
            dve.memset(masks[:, 1, :].rearrange("p (y x) -> p y x", x=WIN)[:, :, WIN // 2:WIN], 1.0)
            dve.memset(masks[:, 2, WS // 2:WS], 1.0).then_inc(mask_step, 1)
            dve.wait_ge(mask_step, 2)
            dve.tensor_scalar(flags[:, :], bits[:, 1:4], 0.0, None, ALU.is_gt).then_inc(mask_step, 1)
            dve.wait_ge(mask_step, 3)
            for v in (1, 2):
                last = dve.tensor_scalar(masks[:, v, :], masks[:, v, :], flags[:, v - 1:v], MASK, ALU.not_equal, ALU.mult)
            dve.tensor_copy(parity_mask[:, 1:2], flags[:, 2:3])
            dve.tensor_scalar(parity_mask[:, 0:1], flags[:, 2:3], -1.0, 1.0, ALU.mult, ALU.add).then_inc(mask_step, 1)
            dve.wait_ge(mask_step, 4)
            dve.tensor_tensor(masks[:, 3, :], masks[:, 1, :], masks[:, 2, :], ALU.min).then_inc(mask_step, 1)
            dve.tensor_copy(ident_r[:, :], ident[:, :])
            dve.tensor_copy(ident_b[:, :], ident[:, :]).then_inc(mask_step, 1)
            dve.wait_ge(mask_step, 6)
            dve.tensor_tensor(pick_max[:, :, :].rearrange("p v (e j) -> p (v e) j", e=2),
                              ident_b[:, 0:16].unsqueeze(2).to_broadcast([128, 16, WS]),
                              ident_b[:, 16:32].unsqueeze(2).to_broadcast([128, 16, WS]), ALU.add)
            dve.wait_ge(setup_pe, 5)
            for v in range(4):
                for e in range(2):
                    half = slice(e * WS, (e + 1) * WS)
                    last = dve.tensor_tensor(
                        bias_sum[half, v, :].rearrange("p (g i) -> p g i", i=WS),
                        pv_ps[half, :, :].rearrange("p b (n h) -> p h (b n)", h=HEADS)[:, e:HEADS:2, :],
                        masks[half, v:v + 1, :].to_broadcast([WS, 2 * QUADS, WS]), ALU.add)
            last.then_inc(setup_dve, 1)
            for b in range(4):
                dve.wait_ge(setup_act, 2 * b + 2)
                for j in range(2):
                    kind = (b % 2) * 2 + j
                    cols = slice(kind * C, (kind + 1) * C)
                    last = dve.scalar_tensor_tensor(w_lo[:, b // 2, cols], banks[b][:, j * C:(j + 1) * C], W_SCALES[kind],
                                                    w_hi[:, b // 2, cols].bitcast(f32), ALU.mult, ALU.subtract)
            last.then_inc(setup_dve, 1)
            dve.wait_ge(setup_act, 9)
            dve.tensor_tensor(b_row[32:33, :], b_raw[32:33, :], b_row[32:33, :].bitcast(f32), ALU.subtract)
            dve.wait_ge(setup_act, 10)
            dve.tensor_tensor(bias_lo[:, :, :], bias_sum, bias_hi[:, :, :].bitcast(f32), ALU.subtract).then_inc(setup_dve, 1)

            def row_stats(row):
                for h in range(HALVES):
                    last = dve.bn_stats(stats[:, bass.ds(row, 1), h, :].rearrange("p a n -> p (a n)"),
                                        one(xc, row)[:, h * ROWTOK:(h + 1) * ROWTOK])
                return last

            with dve.Fori(0, SAMPLES) as s:
                for slot in range(4):
                    dve.wait_ge(in_kept[slot], s + 1)
                    row_stats(s * WROWS + slot).then_inc(stats_done, 1)

            def norm_constants(layer):
                count = [(layer - 1) * NORM_STEPS]

                def step(instruction):
                    instruction.then_inc(norm_dve, 1)
                    count[0] += 1
                    dve.wait_ge(norm_dve, count[0])

                dve.wait_ge(stats_done, layer * ROWS)
                for s in range(SAMPLES):
                    for h in range(HALVES):
                        last = dve.bn_aggr(moments[:, s * HALVES + h, :], stats[:, s * WROWS:(s + 1) * WROWS, h, :])
                step(last)
                dve.wait_ge(norm_pe, 2 * layer - 1)
                dve.tensor_scalar(neg_mean[:, 0:NORMS], proj_ps[:, 0, 0:NORMS], -1.0, None, ALU.mult)
                step(dve.tensor_tensor(tiny[0][:, :], moments[:, :, 0], proj_ps[:, 0, 0:NORMS], ALU.subtract))
                step(dve.tensor_tensor(tiny[1][:, :], tiny[0][:, :], tiny[0][:, :], ALU.mult))
                step(dve.tensor_tensor(tiny[2][:, :], tiny[1][:, :], moments[:, :, 1], ALU.add))
                dve.wait_ge(norm_pe, 2 * layer)
                step(dve.tensor_scalar(tiny[4][:, :], proj_ps[:, 0, NORMS:2 * NORMS], EPS, None, ALU.add))
                dve.wait_ge(norm_act, layer)
                step(dve.reciprocal(tiny[0][:, :], tiny[5][:, :]))
                step(dve.tensor_tensor(tiny[1][:, :], tiny[0][:, :], tiny[4][:, :], ALU.mult))
                step(dve.tensor_tensor(tiny[2][:, :], tiny[1][:, :], tiny[5][:, :], ALU.add))
                step(dve.tensor_scalar(tiny[3][:, :], tiny[2][:, :], 0.5, None, ALU.mult))
                step(dve.reciprocal(rstd[:, 0:NORMS], tiny[3][:, :]))
                dve.tensor_tensor(shift[:, 0:NORMS], neg_mean[:, 0:NORMS], rstd[:, 0:NORMS], ALU.mult).then_inc(norm_ready, 1)
                assert count[0] == layer * NORM_STEPS

            norm_constants(1)

            def q_split(slot, done, spread=0):
                dve.wait_ge(q_flat_done, done)
                wait(dve, q_spread[1 - slot], spread)
                dve.tensor_tensor(q_flat[:, 1, :], proj_ps[:, 0, :], q_flat[:, 0, :], ALU.subtract).then_inc(q_lo_done, 1)
                for g in range(QUADS):
                    rows = slice(32 * g, 32 * g + 32)
                    last = dve.tensor_copy(q_hi[slot][rows, :, :, g, :].rearrange("p h w i -> p (h w) i"),
                                           q_flat[rows, 0, :].rearrange("p (n i) -> p n i", i=WS))
                last.then_inc(q_hi_done, 1)

            def k_low(slot, done):
                dve.wait_ge(k_hi_done, done)
                for e in range(2):
                    last = dve.scalar_tensor_tensor(k_lo[slot][:, :, :, e, :].rearrange("p h w j -> p (h w) j"),
                                                    proj_ps[:, 1, :].rearrange("p (n j) -> p n j", j=WS),
                                                    parity_mask[:, e:e + 1],
                                                    k_hi[slot][:, :, :, e, :].rearrange("p h w j -> p (h w) j"),
                                                    ALU.mult, ALU.subtract)
                last.then_inc(k_lo_done, 1)

            def v_low(slot, done):
                dve.wait_ge(v_hi_done, done)
                for p in range(2):
                    for w in range(2):
                        for e in range(2):
                            rows = slice(e * WS, (e + 1) * WS)
                            last = dve.tensor_tensor(v_lo[2 * slot + p][rows, :, w, :, e, 0:D], v_part(p, w, e),
                                                     v_hi[2 * slot + p][rows, :, w, :, e, 0:D], ALU.subtract)
                last.then_inc(v_lo_done, 1)

            def maxima(n, p):
                dve.wait_ge(max_ps_done, n + 1)
                dve.tensor_reduce(neg_max[:, :], max_ps[:, :, :].rearrange("p w (n j) -> p (w n) j", j=WS), AX.X, ALU.max,
                                  negate=True).then_inc(neg_max_done, 1)
                dve.wait_ge(neg_max_done, n + 1)
                dve.tensor_copy(max_split[p][:, 0:16], neg_max[:, :]).then_inc(max_hi_done, 1)
                dve.wait_ge(max_hi_done, n + 1)
                dve.tensor_tensor(max_split[p][:, 16:32], neg_max[:, :], max_split[p][:, 0:16], ALU.subtract)\
                    .then_inc(max_split_done, 1)

            def attention_out(m, k):
                dve.wait_ge(pv_ps_done, m + 1)
                wait(dve, x1_done, m - 1)
                heads = pv_ps[:, :, 0:2 * WIN_N].rearrange("p h (w n d) -> p h w n d", w=2, d=D + 1)
                dve.reciprocal(recip[:, :, :, :], heads[:, :, :, :, D]).then_inc(recip_done, 1)
                dve.wait_ge(recip_done, m + 1)
                for w in range(2):
                    rows = slice(w * WS, (w + 1) * WS)
                    last = dve.tensor_tensor(attn[k % 2][rows, :, :, :], heads[rows, :, w, :, 0:D],
                                             recip[rows, :, w, :].unsqueeze(3).to_broadcast([WS, HALVES, 2 * QUADS, D]),
                                             ALU.mult)
                last.then_inc(attn_done, 1)

            dve.wait_ge(const_step, 8)
            q_split(0, 1)
            k_low(0, 1)
            v_low(0, 1)
            maxima(0, 0)

            def pair(n, row, k):
                p = k % 2
                nxt = 1 - k // 2
                if not is_last_row(row):
                    if p == 0:
                        q_split(nxt, row + 2, spread_of_row(n, k))
                        k_low(nxt, row + 2)
                    else:
                        v_low(nxt, row + 2)
                if not is_first(n, 1):
                    attention_out(n - 1, (k - 1) % 4)
                if not (isinstance(n, int) and n + 1 >= PAIRS):
                    maxima(n + 1, 1 - p)
                if p == 0 and not is_first(n, 4):
                    dve.wait_ge(x1_kept, n - 2)
                    row_stats(row - 2).then_inc(stats_done, 1)

            run(dve, pair)
            attention_out(PAIRS - 1, 3)
            for back in (2, 1):
                dve.wait_ge(x1_kept, PAIRS + 2 - 2 * back)
                row_stats(ROWS - back).then_inc(stats_done, 1)
            norm_constants(2)

            def lif_units(y):
                for t in range(SAMPLES):
                    m = y * SAMPLES + t
                    h_ps = banks[t % 4]
                    dve.wait_ge(h_ps_done, m + 1)
                    wait(dve, spike_done, y * SAMPLES + (t - 1))
                    if t == 0:
                        dve.tensor_copy(charged[t % 2], h_ps).then_inc(charge_done, 1)
                    else:
                        dve.wait_ge(reset_done, m)
                        dve.scalar_tensor_tensor(charged[t % 2], membrane, 1.0 - 1.0 / TAU, h_ps, ALU.mult, ALU.add)\
                           .then_inc(charge_done, 1)
                    dve.wait_ge(charge_done, m + 1)
                    dve.scalar_tensor_tensor(membrane, charged[t % 2], 1.0, charged[t % 2], ALU.is_lt, ALU.mult)\
                       .then_inc(reset_done, 1)
                    dve.wait_ge(lif_xt_done, m + 1)
                    wait(dve, stored[t % 4], y * 32 + (t // 4) * 16)
                    dve.scalar_tensor_tensor(xstage[:, t % 4, :], charged[t % 2], 1.0, banks[4 + t % 4], ALU.is_ge, ALU.add)\
                       .then_inc(spike_done, 1)

            over_y(dve, lif_units)

        @block.tensor
        def _(pe):
            pe.wait_ge(const_step, 4)
            pe.wait_ge(w_loaded, 32)
            for b in range(4):
                for j in range(4):
                    tile = (b % 2) * 4 + j
                    last = pe.transpose(banks[b][:, j * 128:(j + 1) * 128],
                                        wstage[:, tile, (b // 2) * 128:(b // 2 + 1) * 128], ident[:, :])
                last.then_inc(setup_pe, 1)
            pe.wait_ge(tab_loaded, 16 * 2 * WIN)
            for j in range(2):
                last = pe.matmul(pv_ps[:, j, :], flip[:, :], bias_raw[:, j * 512:(j + 1) * 512], start=True, stop=True)
            last.then_inc(setup_pe, 1)
            pe.wait_ge(setup_dve, 4)
            for v in range(4):
                for j in range(4):
                    last = pe.transpose(banks[4 + v][:, j * 128:(j + 1) * 128], bias_sum[:, v, j * 128:(j + 1) * 128],
                                        ident[:, :])
                last.then_inc(setup_pe, 1)
            pe.wait_ge(setup_dve, 5)

            def turn_sample(s):
                for slot in range(4):
                    pe.wait_ge(in_loaded[slot], (s + 1) * 16)
                    wait(pe, in_kept[slot], s)
                    for h in range(HALVES):
                        for a in range(2):
                            last = pe.transpose(banks[slot][:, h * ROWTOK + a * 128:h * ROWTOK + (a + 1) * 128],
                                                xstage[:, slot, a * C + h * 128:a * C + (h + 1) * 128], ident[:, :])
                    last.then_inc(in_turned[slot], 1)

            turn_sample(0)
            with pe.Fori(1, SAMPLES) as s:
                turn_sample(s)

            def group_averages(layer):
                first = (layer - 1) * NORM_STEPS
                pe.wait_ge(const_step, 6)
                pe.wait_ge(norm_dve, first + 1)
                pe.matmul(proj_ps[:, 0, 0:NORMS], group_avg[:, :], moments[:, :, 0], start=True, stop=True).then_inc(norm_pe, 1)
                pe.wait_ge(norm_dve, first + 4)
                pe.matmul(proj_ps[:, 0, NORMS:2 * NORMS], group_avg[:, :], tiny[2][:, :], start=True, stop=True).then_inc(norm_pe, 1)

            pe.wait_ge(setup_act, SETUP_ACT)
            group_averages(1)

            def project_channels(bank, first, slot):
                for h in range(HALVES):
                    dst = proj_ps[:, bank, h * ROWTOK:(h + 1) * ROWTOK]
                    cols = slice(first + h * 128, first + (h + 1) * 128)
                    pe.matmul(dst, b_row[:, cols], ones_r[:, :], start=True, stop=False)
                    for c in range(HALVES):
                        tok = slice(c * ROWTOK, (c + 1) * ROWTOK)
                        pe.matmul(dst, w_hi[:, c, cols], xn_hi[slot][:, tok], start=False, stop=False)
                        pe.matmul(dst, w_hi[:, c, cols], xn_lo[slot][:, tok], start=False, stop=False)
                        last = pe.matmul(dst, w_lo[:, c, cols], xn_hi[slot][:, tok], start=False, stop=(c == HALVES - 1))
                return last

            def project_tokens(dst, tile, first, slot, bias):
                cols = slice(first, first + C)
                if bias:
                    pe.matmul(dst, ones_r[:, 0:128], b_row[:, cols], start=True, stop=False)
                for c in range(HALVES):
                    tok = slice(c * ROWTOK + tile * 128, c * ROWTOK + (tile + 1) * 128)
                    pe.matmul(dst, xn_hi[slot][:, tok], w_hi[:, c, cols], start=(c == 0 and not bias), stop=False)
                    pe.matmul(dst, xn_hi[slot][:, tok], w_lo[:, c, cols], start=False, stop=False)
                    last = pe.matmul(dst, xn_lo[slot][:, tok], w_hi[:, c, cols], start=False, stop=(c == HALVES - 1))
                return last

            def project_q(slot, r):
                pe.wait_ge(xn_lo_done, r + 1)
                wait(pe, v_lo_done, r)
                project_channels(0, 0, slot).then_inc(q_ps_done, 1)

            def project_k(slot, r):
                wait(pe, x1_kept, 2 * r - 4)
                project_channels(1, C, slot).then_inc(k_ps_done, 1)

            def project_v(slot, r):
                pe.wait_ge(q_lo_done, r + 1)
                for p in range(2):
                    last = project_tokens(proj_ps[:, 0, p * C:(p + 1) * C], p, 2 * C, slot, False)
                last.then_inc(v_ps_done, 1)

            def variant(row, k, w):
                wx = 2 * (k % 2) + w
                at_x = 1 if wx == WCOLS - 1 else 0
                if isinstance(row, int):
                    return 2 * (row % WROWS == WROWS - 1) + at_x
                if k // 2 == 0:
                    return at_x
                return ((row >> 1) & 1) * 2 + at_x

            def table(tensor, v):
                if isinstance(v, int):
                    return tensor[:, v, :]
                return tensor[:, bass.ds(v, 1), :].rearrange("p a n -> p (a n)")

            def max_scores(m, row, k):
                slot = k // 2
                pe.wait_ge(q_hi_done, row + 1)
                pe.wait_ge(k_hi_done, row + 1)
                wait(pe, max_rows_done, m)
                for w in range(2):
                    pe.matmul(max_ps[:, w, :], ident_r[:, :], table(bias_q, variant(row, k, w)), start=True, stop=False)
                    wx = 2 * (k % 2) + w
                    for h in range(HALVES):
                        for mid in range(2):
                            at = (2 * h + mid) * 128
                            last = pe.matmul(max_ps[:, w, at:at + 128],
                                             q_hi[slot][:, h, wx, 2 * mid:2 * mid + 2, :].rearrange("p q i -> p (q i)"),
                                             k_hi[slot][:, h, wx, :, :].rearrange("p e j -> p (e j)"),
                                             start=False, stop=(h == 1 and mid == 1))
                last.then_inc(max_ps_done, 1)

            def scores(n, row, k):
                slot, p = k // 2, k % 2
                pe.wait_ge(k_lo_done, row + 1)
                pe.wait_ge(q_spread[slot], spread_of_row(n, k))
                for w in range(2):
                    wx = 2 * p + w
                    wait(pe, p_hi_done, n * 2 + (w - 1))
                    v = variant(row, k, w)
                    pe.matmul(score_ps[:, w, :], ident_r[:, :], table(bias_hi, v), start=True, stop=False)
                    pe.matmul(score_ps[:, w, :], ident_r[:, :], table(bias_lo, v), start=False, stop=False)
                    for h in range(HALVES):
                        dst = score_ps[:, w, h * 256:(h + 1) * 256]
                        at_q = (h * WCOLS + wx) * WS
                        high = q_hi[slot][:, h, wx, :, :].rearrange("p q i -> p (q i)")
                        for keys, queries in ((k_hi, high), (k_hi, q_lo[slot][:, :, at_q:at_q + WS]), (k_lo, high)):
                            pe.matmul(dst, keys[slot][:, h, wx, :, :].rearrange("p e j -> p (e j)"), queries,
                                      start=False, stop=False)
                    if w == 0:
                        turn_maxima(n, p)
                pe.wait_ge(max_rows_done, n + 1)
                for w in range(2):
                    for b in range(4):
                        last = pe.matmul(score_ps[:, w, b * 128:(b + 1) * 128], pick_max[:, 4 * w + b, :], max_rows[p][:, :],
                                         start=False, stop=(b == 3))
                    last.then_inc(score_ps_done, 1)

            def turn_maxima(n, p):
                pe.wait_ge(max_split_done, n + 1)
                pe.transpose(max_ps[:, 0, :].bitcast(bf16)[0:32, 0:128], max_split[p][:, :], ident_b[:, :])\
                  .then_inc(max_turned, 1)

            def weigh_values(m, row, k):
                p = k % 2
                pe.wait_ge(p_lo_done, m * 2 + 2)
                pe.wait_ge(v_lo_done, row + 1)
                wait(pe, attn_done, m)
                for h in range(HALVES):
                    cols = pv_ps[:, h, 0:2 * WIN_N].rearrange("p (w g n) -> p w g n", w=2, g=QUADS)
                    for g in range(QUADS):
                        for at, (pp, vv) in enumerate(((p_hi, v_hi), (p_hi, v_lo), (p_lo, v_hi))):
                            last = pe.matmul(cols[:, :, g, :], pp[p][:, h * QUADS + g, :, :].rearrange("p w i -> p (w i)"),
                                             vv[k][:, h, :, g, :, :].rearrange("p w e d -> p w (e d)"),
                                             start=(at == 0), stop=(at == 2))
                last.then_inc(pv_ps_done, 1)

            def turn_x1(m, k):
                pe.wait_ge(x1_done, m + 1)
                wait(pe, x1_kept, m)
                for h in range(HALVES):
                    last = pe.transpose(proj_ps[:, 1, h * 128:(h + 1) * 128], x1[k % 2][:, h * 128:(h + 1) * 128],
                                        ident[:, :])
                last.then_inc(x1_turned, 1)

            pe.wait_ge(setup_dve, SETUP_DVE)
            project_q(0, 0)
            project_k(0, 0)
            project_v(0, 0)
            max_scores(0, 0, 0)

            def pair(n, row, k):
                p = k % 2
                nxt = 1 - k // 2
                if not is_last_row(row):
                    if p == 0:
                        project_q(nxt, row + 1)
                        project_k(nxt, row + 1)
                    else:
                        project_v(nxt, row + 1)
                scores(n, row, k)
                if not is_first(n, 1):
                    weigh_values(n - 1, row if p else row - 1, (k - 1) % 4)
                if not (isinstance(n, int) and n + 1 >= PAIRS):
                    max_scores(n + 1, row + 1 if p else row, (k + 1) % 4)
                if not is_first(n, 2):
                    if p == 0 and not is_last_row(row):
                        pe.wait_ge(k_lo_done, row + 2)
                    turn_x1(n - 2, k)

            run(pe, pair)
            weigh_values(PAIRS - 1, ROWS - 1, 3)
            turn_x1(PAIRS - 2, 0)
            turn_x1(PAIRS - 1, 1)
            pe.wait_ge(x1_kept, PAIRS)
            group_averages(2)
            pe.wait_ge(norm_ready, 2)

            def lif_units(y):
                for t in range(SAMPLES):
                    m = y * SAMPLES + t
                    s = t % 4
                    pe.wait_ge(lif_loaded[s], y * 32 + (t // 4 + 1) * 16)
                    wait(pe, spike_done, y * SAMPLES + (t - 3))
                    for h in range(HALVES):
                        for a in range(2):
                            last = pe.transpose(banks[4 + s][:, a * C + h * 128:a * C + (h + 1) * 128],
                                                lif_x[s][:, h * ROWTOK + a * 128:h * ROWTOK + (a + 1) * 128], ident[:, :])
                    last.then_inc(lif_xt_done, 1)
                    pe.wait_ge(xn_lo_done, y * SAMPLES + (ROWS + t + 1))
                    for a in range(2):
                        last = project_tokens(banks[s][:, a * C:(a + 1) * C], a, 3 * C, t % 2, True)
                    last.then_inc(h_ps_done, 1)

            over_y(pe, lif_units)


_INS = ['x', 'L0_conv_qkv_w', 'L0_conv_qkv_b', 'L0_conv_bias_table', 'L1_conv_W', 'L1_conv_b']


def kernel(**inputs):
    import numpy as _np
    import concourse.bacc as _bacc
    from concourse import mybir as _mybir
    from concourse.bass_utils import run_bass_kernel_spmd as _run

    nc = _bacc.Bacc("TRN2", target_bir_lowering=False, num_devices=1)
    arrays, args = {}, []
    for name in _INS:
        a = _np.ascontiguousarray(inputs[name])
        arrays[f"in_{name}_dram"] = a
        args.append(nc.dram_tensor(f"in_{name}_dram", a.shape, _mybir.dt.from_np(a.dtype), kind="ExternalInput").ap())
    shape = arrays["in_x_dram"].shape
    args.append(nc.dram_tensor("out_0_dram", shape, _mybir.dt.float32, kind="ExternalOutput").ap())
    swin_attention_then_lif_kernel(nc, *args)
    r = _run(nc, [arrays], core_ids=[0])
    return r.results[0]["out_0_dram"]
```

```python
import concourse.bass as bass
from concourse import mybir
from contextlib import ExitStack


def swin_attention_then_lif_kernel(nc, image, x, qkv_w, qkv_b, bias_table, lif_w, lif_b, out):
    f32, f32r = mybir.dt.float32, mybir.dt.float32r
    f16, bf16, i32 = mybir.dt.float16, mybir.dt.bfloat16, mybir.dt.int32
    ALU = mybir.AluOpType
    ACT = mybir.ActivationFunctionType
    AX = mybir.AxisListType

    SAMPLES, HEIGHT, WIDTH, C = image
    WIN = 8
    WS = WIN * WIN
    HEADS = bias_table.shape[1]
    D = C // HEADS
    HALVES = C // 128
    WROWS = HEIGHT // WIN
    WCOLS = WIDTH // WIN
    ROWS = SAMPLES * WROWS
    PAIRS = ROWS * 2
    ROWTOK = WCOLS * WS
    QUADS = 4
    QK_SCALE = float(D) ** -0.5
    TAU = 2.0
    EPS = 1e-5
    GROUP = C // 32
    MASK = -100.0
    OUTS = 3 * C + C
    PV_N = 2 * (D + 1)
    WIN_N = QUADS * PV_N

    ctx = ExitStack()
    with ctx:
        def sb(name, shape, dt):
            return ctx.enter_context(nc.sbuf_tensor(name, shape, dt))

        def sem(name):
            return ctx.enter_context(nc.semaphore(name))

        xc = sb("xc", [128, ROWS, HALVES * ROWTOK], f32)
        w_hi = sb("w_hi", [128, HALVES, OUTS], f32r)
        w_lo = sb("w_lo", [128, HALVES, OUTS], f32r)
        b_row = sb("b_row", [128, C], f32r)
        b_cols = sb("b_cols", [128, 3 * HALVES], f32)
        ones_r = sb("ones_r", [128, ROWTOK], f32r)
        ident = sb("ident", [128, 128], f32)
        ident_r = sb("ident_r", [128, 128], f32r)
        ident_b = sb("ident_b", [128, 128], bf16)
        group_avg = sb("group_avg", [128, 128], f32)
        parity_mask = sb("parity_mask", [128, 2], f32)
        pick_max = sb("pick_max", [128, 2 * QUADS, 128], bf16)
        bias_hi = sb("bias_hi", [128, 4, 512], f32r)
        bias_lo = sb("bias_lo", [128, 4, 512], f32r)
        bias_q = sb("bias_q", [128, 4, 512], f32r)
        x_stats = sb("x_stats", [128, WROWS, HALVES, 6], f32)
        x1_stats = sb("x1_stats", [128, ROWS, HALVES, 6], f32)
        moments = sb("moments", [128, SAMPLES * HALVES, 2], f32)
        neg_mean = sb("neg_mean", [128, (SAMPLES + 1) * HALVES], f32)
        rstd = sb("rstd", [128, (SAMPLES + 1) * HALVES], f32)
        shift = sb("shift", [128, (SAMPLES + 1) * HALVES], f32)
        tiny = [sb(f"tiny{i}", [128, SAMPLES * HALVES], f32) for i in range(8)]
        root_guess = sb("root_guess", [128, SAMPLES * HALVES], i32)
        three_halves = sb("three_halves", [128, SAMPLES * HALVES], f32)

        w_raw = sb("w_raw", [128, HALVES, OUTS], f32)
        bias_sum = w_raw[:, :, :].rearrange("p h n -> p (h n)").rearrange("p (v n) -> p v n", v=4)
        bias_raw = sb("bias_raw", [WS, WS * HEADS], f32)
        flip = sb("flip", [WS, 128], f32)
        masks = sb("masks", [128, 4, WS], f32)
        bits = sb("bits", [128, 4], i32)
        flags = sb("flags", [128, 3], f32)
        xn = [sb(f"xn{i}", [128, HALVES * ROWTOK], f32) for i in range(2)]
        xn_hi = [sb(f"xn_hi{i}", [128, HALVES * ROWTOK], f32r) for i in range(2)]
        xn_lo = [sb(f"xn_lo{i}", [128, HALVES * ROWTOK], f32r) for i in range(2)]
        q_flat = sb("q_flat", [128, 2, HALVES * ROWTOK], f16)
        k_flat = sb("k_flat", [128, 2, HALVES * ROWTOK], f16)
        q_hi = [sb(f"q_hi{i}", [128, HALVES, WCOLS, QUADS, WS], f16) for i in range(2)]
        q_lo = [sb(f"q_lo{i}", [128, QUADS, HALVES * ROWTOK], f16) for i in range(2)]
        k_hi = [sb(f"k_hi{i}", [128, HALVES, WCOLS, 2, WS], f16) for i in range(2)]
        k_lo = [sb(f"k_lo{i}", [128, HALVES, WCOLS, 2, WS], f16) for i in range(2)]
        v_hi = [sb(f"v_hi{i}", [128, HALVES, 2, QUADS, 2, D + 1], f16) for i in range(4)]
        v_lo = [sb(f"v_lo{i}", [128, HALVES, 2, QUADS, 2, D + 1], f16) for i in range(4)]
        probs = sb("probs", [128, 2 * QUADS, 2, WS], f32)
        p_hi = [sb(f"p_hi{i}", [128, 2 * QUADS, 2, WS], f16) for i in range(2)]
        p_lo = [sb(f"p_lo{i}", [128, 2 * QUADS, 2, WS], f16) for i in range(2)]
        neg_max = sb("neg_max", [128, 16], f32)
        max_split = [sb(f"max_split{i}", [128, 32], bf16) for i in range(2)]
        max_rows = [sb(f"max_rows{i}", [128, 128], bf16) for i in range(2)]
        b_raw = probs[:, :, :, :].rearrange("p g w i -> p (g w i)")[:, 0:C]
        recip = sb("recip", [128, HALVES, 2, 2 * QUADS], f32)
        attn = [sb(f"attn{i}", [128, HALVES, 2 * QUADS, D], f32) for i in range(2)]
        attn_cm = [sb(f"attn_cm{i}", [128, HALVES, 128], f32) for i in range(2)]
        unit_hi = [bias_hi[:, i, :] for i in range(4)]
        unit_lo = [bias_lo[:, i, :] for i in range(4)]
        charged = [sb(f"charged{i}", [128, HALVES * ROWTOK], f32) for i in range(2)]
        first_charge = probs[:, :, :, :].rearrange("p g w i -> p (g w i)")[:, 0:HALVES * ROWTOK]
        membrane = sb("membrane", [128, HALVES * ROWTOK], f32)

        max_ps, score_ps, pv_ps, proj_ps = [
            ctx.enter_context(nc.psum_tensor(name, [128, 2, 512], f32))
            for name in ("max_ps", "score_ps", "pv_ps", "proj_ps")]
        banks = [t[:, j, :] for t in (max_ps, score_ps, pv_ps, proj_ps) for j in range(2)]

        w_loaded = sem("w_loaded")
        tab_loaded = sem("tab_loaded")
        b_loaded = sem("b_loaded")
        const_step = sem("const_step")
        setup_pe = sem("setup_pe")
        setup_act = sem("setup_act")
        setup_dve = sem("setup_dve")
        masked = sem("masked")
        mask_step = sem("mask_step")
        first_loaded = [sem(f"first_loaded{i}") for i in range(4)]
        x_loaded = sem("x_loaded")
        x_stats_done = sem("x_stats_done")
        x1_stats_done = sem("x1_stats_done")
        norm_pe = sem("norm_pe")
        norm_dve = sem("norm_dve")
        root_dve = sem("root_dve")
        root_pool = sem("root_pool")
        norm_ready = sem("norm_ready")
        xn_done = sem("xn_done")
        xn_hi_done = sem("xn_hi_done")
        xn_lo_done = sem("xn_lo_done")
        q_ps_done = sem("q_ps_done")
        k_ps_done = sem("k_ps_done")
        v_ps_done = sem("v_ps_done")
        q_flat_done = sem("q_flat_done")
        k_flat_done = sem("k_flat_done")
        k_ps_read = sem("k_ps_read")
        q_hi_done = sem("q_hi_done")
        k_hi_done = sem("k_hi_done")
        v_hi_done = sem("v_hi_done")
        q_lo_done = sem("q_lo_done")
        q_spread = [sem(f"q_spread{i}") for i in range(2)]
        k_lo_done = sem("k_lo_done")
        v_lo_done = sem("v_lo_done")
        max_ps_done = sem("max_ps_done")
        neg_max_done = sem("neg_max_done")
        max_hi_done = sem("max_hi_done")
        max_split_done = sem("max_split_done")
        max_turned = sem("max_turned")
        max_rows_done = sem("max_rows_done")
        score_ps_done = sem("score_ps_done")
        p_hi_done = sem("p_hi_done")
        p_lo_done = sem("p_lo_done")
        pv_ps_done = sem("pv_ps_done")
        recip_done = sem("recip_done")
        attn_done = sem("attn_done")
        attn_turned = sem("attn_turned")
        attn_kept = sem("attn_kept")
        x1_done = sem("x1_done")
        h_ps_done = sem("h_ps_done")
        first_done = sem("first_done")
        charge_done = sem("charge_done")
        reset_done = sem("reset_done")
        spike_done = sem("spike_done")
        stored = sem("stored")

        def wait(eng, s, value):
            if not isinstance(value, int) or value > 0:
                eng.wait_ge(s, value)

        def one(tensor, row):
            return tensor[:, bass.ds(row, 1), :].rearrange("p a n -> p (a n)")

        def run(eng, body):
            for k in range(BODY):
                body(k, k // 2, k, 0)
            with eng.Fori(1, SAMPLES - 2) as s:
                for k in range(BODY):
                    body(s * BODY + k, s * WROWS + k // 2, k, s)
            for s in (SAMPLES - 2, SAMPLES - 1):
                for k in range(BODY):
                    body(s * BODY + k, s * WROWS + k // 2, k, s)

        def times_slots(n, k, per):
            return (n + (4 - k % 4)) * (per // 4)

        def has_sample(s, ahead):
            return not isinstance(s, int) or s + ahead < SAMPLES

        def is_first(n, lag):
            return isinstance(n, int) and n < lag

        def norm_beside(s, k):
            if has_sample(s, 1):
                return s + 1, (s + 1) * HALVES, HALVES, k - 1
            return SAMPLES, 0, EARLY, k - 3

        def norm_roots(eng, step_done, before, norm, first, width):
            cols = bass.ds(first, width)
            half, product, factor = (tiny[i][:, 0:width] for i in (3, 6, 7))
            roots = [root_guess[:, 0:width].bitcast(f32), tiny[4][:, 0:width], tiny[5][:, 0:width], rstd[:, cols]]
            eng.wait_ge(norm_dve, norm * NORM_STEPS + NORM_STEPS)
            for i in range(NEWTONS):
                done = before + 4 * i
                eng.tensor_tensor(product, roots[i], roots[i], ALU.mult).then_inc(step_done, 1)
                eng.wait_ge(step_done, done + 1)
                eng.tensor_tensor(factor, product, half, ALU.mult).then_inc(step_done, 1)
                eng.wait_ge(step_done, done + 2)
                eng.tensor_tensor(product, three_halves[:, 0:width], factor, ALU.subtract).then_inc(step_done, 1)
                eng.wait_ge(step_done, done + 3)
                eng.tensor_tensor(roots[i + 1], roots[i], product, ALU.mult).then_inc(step_done, 1)
                eng.wait_ge(step_done, done + 4)
            eng.tensor_tensor(shift[:, cols], neg_mean[:, cols], rstd[:, cols], ALU.mult).then_inc(norm_ready, 1)

        def is_last_pair(n):
            return isinstance(n, int) and n == PAIRS - 1

        def is_last_row(row, ahead=1):
            return isinstance(row, int) and row + ahead >= ROWS

        def is_last_y(y):
            return isinstance(y, int) and y == WROWS - 1

        def over_y(eng, body):
            body(0)
            with eng.Fori(1, WROWS - 1) as y:
                body(y)
            body(WROWS - 1)

        BODY = 2 * WROWS
        W_SCALES = ((0, C, QK_SCALE), (C, 3 * C, 1.0), (3 * C, OUTS, 1.0 / TAU))

        NORMS = SAMPLES * HALVES
        EARLY = NORMS - HALVES
        NEWTONS = 3
        NORM_STEPS = 6
        ROOT_STEPS = 4 * NEWTONS
        SETUP_DVE = 6
        SETUP_ACT = 12

        def v_part(p, w, e):
            return proj_ps[w * WS:(w + 1) * WS, 0, p * C:(p + 1) * C]\
                .rearrange("p (h g e d) -> p h g e d", h=HALVES, g=QUADS, e=2)[:, :, :, e, :]

        free_averages = proj_ps[:, 0, 0:2 * NORMS]
        spare_averages = pv_ps[:, 0, 512 - 2 * NORMS:512]

        block = ctx.enter_context(nc.Block())

        @block.sync
        def _(sp):
            for y in range(WROWS):
                sp.dma_start(xc[:, y, :], x[0, :, y, :]).then_inc(first_loaded[y], 16)
            sp.dma_start(w_raw[:, :, 0:3 * C], qkv_w.rearrange("(h p) n -> p h n", p=128)).then_inc(w_loaded, 16)
            sp.dma_start(w_raw[:, :, 3 * C:OUTS], lif_w.rearrange("(h p) n -> p h n", p=128)).then_inc(w_loaded, 16)
            span = 2 * WIN - 1
            for yj in range(WIN):
                src = bass.AP(tensor=bias_table.tensor, offset=yj * span * HEADS,
                              ap=[[HEADS, WIN], [span * HEADS, WIN], [1, WIN * HEADS]])
                sp.dma_start(bias_raw[yj * WIN:(yj + 1) * WIN, :], src).then_inc(tab_loaded, 16)
            for y in range(WROWS):
                sp.dma_start(xc[:, WROWS + y, :], x[1, :, y, :]).then_inc(x_loaded, 16)

            def spread_q(slot, done):
                sp.wait_ge(q_lo_done, done)
                for g in range(QUADS):
                    rows = slice(32 * g, 32 * g + 32)
                    sp.dma_start(q_lo[slot][rows, g, :], q_flat[rows, 1, :]).then_inc(q_spread[slot], 16)

            sp.wait_ge(const_step, 10)
            spread_q(0, 1)

            def pair(n, row, k, s):
                if k % 2 == 0 and has_sample(s, 2):
                    sp.wait_ge(x_loaded, row * 16 + WROWS * 16)
                    sp.dma_start(one(xc, row + 2 * WROWS), x[bass.ds(s + 2, 1), :, k // 2, :].rearrange("s p n -> (s p) n"))\
                      .then_inc(x_loaded, 16)
                if k % 2 == 0 and not is_last_row(row):
                    spread_q((k // 2 + 1) % 2, row + 2)

            run(sp, pair)

            def store_units(y):
                for t in range(SAMPLES):
                    sp.wait_ge(spike_done, y * SAMPLES + (t + 1))
                    sp.dma_start(out[t, :, bass.ds(y, 1), :].rearrange("p y n -> p (y n)"), one(xc, y + t * WROWS))\
                      .then_inc(stored, 16)

            over_y(sp, store_units)
            sp.wait_ge(stored, 16 * ROWS)

        @block.gpsimd
        def _(pool):
            pool.memset(ident[:, :], 0.0).then_inc(const_step, 1)
            pool.memset(flip[:, :], 0.0)
            pool.memset(group_avg[:, :], 1.0 / GROUP).then_inc(const_step, 1)
            pool.iota(bits[:, 0:1], pattern=[[0, 1]], base=0, channel_multiplier=1).then_inc(const_step, 1)
            pool.wait_ge(const_step, 3)
            pool.affine_select(out=ident[:, :], in_=ident[:, :], compare_op=ALU.not_equal, fill=1.0, base=0,
                               pattern=[[-1, 128]], channel_multiplier=1)
            turned = flip[:, :].rearrange("p (e j) -> p e j", e=2)
            pool.affine_select(out=turned, in_=turned, compare_op=ALU.not_equal, fill=1.0, base=1 - WS,
                               pattern=[[0, 2], [1, WS]], channel_multiplier=1).then_inc(const_step, 1)
            grp = group_avg[:, :].rearrange("p (g e) -> p g e", e=GROUP)
            pool.affine_select(out=grp, in_=grp, compare_op=ALU.is_ge, fill=0.0, base=0,
                               pattern=[[-GROUP, 128 // GROUP], [0, GROUP]], channel_multiplier=1).then_inc(const_step, 1)
            pool.wait_ge(const_step, 5)
            pool.affine_select(out=grp, in_=grp, compare_op=ALU.is_ge, fill=0.0, base=GROUP - 1,
                               pattern=[[GROUP, 128 // GROUP], [0, GROUP]], channel_multiplier=-1).then_inc(const_step, 1)

            for buf in (q_hi[0], k_hi[0], k_lo[0]):
                pool.memset(buf[:, :, :, :, :], 0.0)
            pool.memset(q_lo[0][:, :, :], 0.0)
            for buf in v_hi[0:2] + v_lo[0:2]:
                pool.memset(buf[:, :, :, :, :, :], 0.0)
            for buf in max_rows:
                zeroed = pool.memset(buf[:, :], 0.0)
            zeroed.then_inc(const_step, 1)

            def ones_of_values(buffers):
                for buf in buffers:
                    for e in range(2):
                        for h in range(HALVES):
                            last = pool.memset(buf[e * WS:(e + 1) * WS, h, :, :, e, D:D + 1], 1.0)
                return last

            pool.wait_ge(const_step, 7)
            ones_of_values(v_hi[0:2]).then_inc(const_step, 1)
            pool.wait_ge(const_step, 8)
            pool.memset(q_hi[1][:, :, :, :, :], 0.0)
            pool.memset(q_lo[1][:, :, :], 0.0)

            def low_part(slot, done, high=None, low=None):
                high, low = (xn_hi[slot][:, :], xn_lo[slot][:, :]) if high is None else (high, low)
                pool.wait_ge(xn_hi_done, done)
                pool.tensor_tensor(low, xn[slot][:, :], high.bitcast(f32), ALU.subtract)\
                    .then_inc(xn_lo_done, 1)

            low_part(0, 1)
            for buf in (k_hi[1], k_lo[1]):
                zeroed = pool.memset(buf[:, :, :, :, :], 0.0)
            zeroed.then_inc(const_step, 1)
            pool.wait_ge(const_step, 9)
            pool.wait_ge(setup_dve, 3)
            ones_of_values(v_hi[2:4]).then_inc(const_step, 1)
            pool.wait_ge(const_step, 10)
            pool.wait_ge(mask_step, 5)
            pool.wait_ge(setup_dve, 5)
            for v in range(1, 4):
                pool.tensor_tensor(bias_sum[:, v, :].rearrange("p (g i) -> p g i", i=WS),
                                   bias_sum[:, 0, :].rearrange("p (g i) -> p g i", i=WS),
                                   masks[:, v:v + 1, :].to_broadcast([128, 2 * QUADS, WS]), ALU.add).then_inc(masked, 1)
            low_part(1, 2)

            def add_attention(m, row, p):
                pool.wait_ge(attn_kept, m + 1)
                tokens = one(xc, row).rearrange("p (h n) -> p h n", h=HALVES)[:, :, p * 128:(p + 1) * 128]
                pool.tensor_tensor(tokens, tokens, attn_cm[p][:, :, :], ALU.add).then_inc(x1_done, 1)

            def pair(n, row, k, s):
                p = k % 2
                if p == 1 and not is_last_row(row, 2):
                    low_part(k // 2 % 2, row + 3)
                if is_last_pair(n):
                    low_part(0, ROWS + 1, unit_hi[0], unit_lo[0])
                wait(pool, pv_ps_done, n - 1)
                for w in range(2):
                    pool.wait_ge(p_hi_done, n * 2 + (w + 1))
                    pool.tensor_tensor(p_lo[p][:, :, w, :], probs[:, :, w, :], p_hi[p][:, :, w, :], ALU.subtract)\
                        .then_inc(p_lo_done, 1)
                if not is_first(n, 2):
                    add_attention(n - 2, row - 1, p)
                norm, first, width, stage = norm_beside(s, k)
                if stage == 1:
                    norm_roots(pool, root_pool, (norm - 1) * ROOT_STEPS, norm, first, width)

            run(pool, pair)

            def lif_units(y):
                for t in range(SAMPLES):
                    if not (is_first(y, 1) and t == 0):
                        low_part(t % 2, y * SAMPLES + (ROWS + t + 1), unit_hi[t % 4], unit_lo[t % 4])
                    if is_first(y, 1) and t == 1:
                        for p in range(2):
                            add_attention(PAIRS - 2 + p, ROWS - 1, p)
                    if is_first(y, 1) and t == 4:
                        norm_roots(pool, root_pool, SAMPLES * ROOT_STEPS, SAMPLES + 1, EARLY, HALVES)

            over_y(pool, lif_units)

        @block.scalar
        def _(act):
            act.dma_start(b_cols[:, :], qkv_b).then_inc(b_loaded, 16)
            act.wait_ge(setup_dve, 1)
            for r in (0, 32):
                act.dma_start(b_raw[r:r + 1, :], lif_b.rearrange("(o c) -> o c", o=1)).then_inc(b_loaded, 16)

            def normalise(row, sample, slot, norm, done):
                act.wait_ge(norm_ready, norm)
                wait(act, xn_lo_done, done - 1)
                for h in range(HALVES):
                    col = bass.ds(sample * HALVES + h, 1)
                    last = act.activation(xn[slot][:, h * ROWTOK:(h + 1) * ROWTOK],
                                          one(xc, row)[:, h * ROWTOK:(h + 1) * ROWTOK], ACT.Identity,
                                          bias=shift[:, col], scale=rstd[:, col])
                last.then_inc(xn_done, 1)

            def xn_high(slot, done, high=None):
                high = xn_hi[slot][:, :] if high is None else high
                act.wait_ge(xn_done, done)
                act.activation(high, xn[slot][:, :], ACT.Copy).then_inc(xn_hi_done, 1)

            def with_bias(flat, first):
                for h in range(HALVES):
                    tok = slice(h * ROWTOK, (h + 1) * ROWTOK)
                    last = act.activation(flat[:, 0, tok], proj_ps[:, first // 2, tok], ACT.Identity,
                                          bias=b_cols[:, first + h:first + h + 1])
                return last

            def q_high(done):
                act.wait_ge(q_ps_done, done)
                wait(act, q_hi_done, done - 1)
                with_bias(q_flat, 0).then_inc(q_flat_done, 1)

            def k_high(done):
                act.wait_ge(k_ps_done, done)
                wait(act, k_hi_done, done - 1)
                with_bias(k_flat, HALVES).then_inc(k_flat_done, 1)

            def v_high(slot, done):
                act.wait_ge(v_ps_done, done)
                for p in range(2):
                    for w in range(2):
                        for e in range(2):
                            last = act.activation(v_hi[2 * slot + p][e * WS:(e + 1) * WS, :, w, :, e, 0:D],
                                                  v_part(p, w, e), ACT.Copy)
                last.then_inc(v_hi_done, 1)

            act.wait_ge(w_loaded, 32)
            for first, end, scale in W_SCALES:
                act.activation(w_hi[:, :, first:end], w_raw[:, :, first:end], ACT.Copy, scale=scale).then_inc(setup_act, 1)
            normalise(0, 0, 0, 1, 0)
            xn_high(0, 1)
            normalise(1, 0, 1, 1, 1)
            act.wait_ge(setup_dve, 3)
            q_high(1)
            k_high(1)
            act.wait_ge(const_step, 8)
            v_high(0, 1)
            xn_high(1, 2)
            for v in range(4):
                act.wait_ge(setup_pe, 2 + v)
                act.activation(bias_q[:, v, :], banks[4 + v % 2], ACT.Copy).then_inc(setup_act, 1)
            act.activation(b_row[:, :], b_raw, ACT.Copy).then_inc(setup_act, 1)
            for v in range(4):
                act.activation(bias_hi[:, v, :], bias_sum[:, v, :], ACT.Copy).then_inc(setup_act, 1)
            act.wait_ge(const_step, 10)

            def keep_attention(m, p):
                wait(act, x1_done, m - 1)
                act.wait_ge(attn_turned, m + 1)
                for h in range(HALVES):
                    last = act.activation(attn_cm[p][:, h, :], proj_ps[:, 1, h * 128:(h + 1) * 128], ACT.Identity,
                                          bias=b_cols[:, 2 * HALVES + h:2 * HALVES + h + 1])
                last.then_inc(attn_kept, 1)

            def unit_normed(y, t):
                normalise(y + t * WROWS, t, t % 2, SAMPLES + (2 if t == SAMPLES - 1 else 1), y * SAMPLES + (ROWS + t))

            def pair(n, row, k, s):
                p = k % 2
                nxt = (k // 2 + 1) % 2
                if is_last_pair(n):
                    unit_normed(0, 0)
                if not is_last_row(row):
                    if p == 0:
                        q_high(row + 2)
                        k_high(row + 2)
                    else:
                        v_high(nxt, row + 2)
                if p == 1 and not is_last_row(row, 2):
                    xn_high(1 - nxt, row + 3)
                act.wait_ge(max_turned, n + 1)
                act.activation(max_rows[p][0:32, :], max_ps[:, 0, :].bitcast(bf16)[0:32, 0:128], ACT.Copy)\
                    .then_inc(max_rows_done, 1)
                if is_last_pair(n):
                    xn_high(0, ROWS + 1, unit_hi[0])
                if p == 0 and not is_last_row(row, 2):
                    sample = s + (k // 2 + 2) // WROWS
                    normalise(row + 2, sample, 1 - nxt, sample + 1, row + 2)
                wait(act, pv_ps_done, n - 1)
                for w in range(2):
                    wait(act, p_lo_done, n * 2 + (w - 1))
                    act.wait_ge(score_ps_done, n * 2 + (w + 1))
                    scores = score_ps[:, w, :].rearrange("p (g i) -> p g i", i=WS)
                    act.activation(probs[:, :, w, :], scores, ACT.Exp)
                    act.activation(p_hi[p][:, :, w, :], scores, ACT.Exp).then_inc(p_hi_done, 1)
                if not is_first(n, 2):
                    keep_attention(n - 2, p)

            run(act, pair)

            def lif_units(y):
                for t in range(SAMPLES):
                    m = y * SAMPLES + t
                    if not (is_first(y, 1) and t == 0):
                        wait(act, h_ps_done, m - 3)
                        xn_high(t % 2, m + (ROWS + 1), unit_hi[t % 4])
                    if t == (1 if is_first(y, 1) else 2):
                        act.wait_ge(p_lo_done, 2 * PAIRS)
                        act.wait_ge(h_ps_done, y * SAMPLES + 1)
                        act.activation(first_charge, banks[0], ACT.Copy).then_inc(first_done, 1)
                    if is_first(y, 1) and t == 1:
                        for p in range(2):
                            keep_attention(PAIRS - 2 + p, p)
                    if t + 1 < SAMPLES:
                        unit_normed(y, t + 1)
                    elif not is_last_y(y):
                        unit_normed(y + 1, 0)

            over_y(act, lif_units)

        @block.vector
        def _(dve):
            dve.memset(b_raw, 0.0).then_inc(setup_dve, 1)
            dve.memset(ones_r[:, :].bitcast(f32), 1.0)
            dve.memset(three_halves[:, :], 1.5)
            dve.memset(masks[:, :, :], 0.0).then_inc(setup_dve, 1)
            dve.wait_ge(const_step, 4)
            for j, bit in enumerate((4, 32, 16)):
                last = dve.tensor_scalar(bits[:, j + 1:j + 2], bits[:, 0:1], bit, None, ALU.bitwise_and)
            last.then_inc(mask_step, 1)
            dve.wait_ge(setup_dve, 2)
            dve.memset(masks[:, 1, :].rearrange("p (y x) -> p y x", x=WIN)[:, :, WIN // 2:WIN], 1.0)
            dve.memset(masks[:, 2, WS // 2:WS], 1.0).then_inc(mask_step, 1)
            dve.wait_ge(mask_step, 2)
            dve.tensor_scalar(flags[:, :], bits[:, 1:4], 0.0, None, ALU.is_gt).then_inc(mask_step, 1)
            dve.wait_ge(mask_step, 3)
            for v in (1, 2):
                last = dve.tensor_scalar(masks[:, v, :], masks[:, v, :], flags[:, v - 1:v], MASK, ALU.not_equal, ALU.mult)
            dve.tensor_copy(parity_mask[:, 1:2], flags[:, 2:3])
            dve.tensor_scalar(parity_mask[:, 0:1], flags[:, 2:3], -1.0, 1.0, ALU.mult, ALU.add).then_inc(mask_step, 1)
            dve.wait_ge(mask_step, 4)
            dve.tensor_tensor(masks[:, 3, :], masks[:, 1, :], masks[:, 2, :], ALU.min).then_inc(mask_step, 1)
            dve.tensor_copy(ident_r[:, :], ident[:, :])
            dve.tensor_copy(ident_b[:, :], ident[:, :]).then_inc(mask_step, 1)
            dve.wait_ge(mask_step, 6)
            dve.tensor_tensor(pick_max[:, :, :].rearrange("p v (e j) -> p (v e) j", e=2),
                              ident_b[:, 0:16].unsqueeze(2).to_broadcast([128, 16, WS]),
                              ident_b[:, 16:32].unsqueeze(2).to_broadcast([128, 16, WS]), ALU.add)
            for buf in v_hi[2:4] + v_lo[2:4]:
                dve.memset(buf[:, :, :, :, :, :], 0.0)
            dve.wait_ge(b_loaded, 48)
            dve.tensor_scalar(b_cols[:, 0:HALVES], b_cols[:, 0:HALVES], QK_SCALE, None, ALU.mult)
            for r in (0, 32):
                last = dve.tensor_scalar(b_raw[r:r + 1, :], b_raw[r:r + 1, :], 1.0 / TAU, None, ALU.mult)
            last.then_inc(setup_dve, 1)

            def row_stats(stats, at, row):
                for h in range(HALVES):
                    last = dve.bn_stats(stats[:, bass.ds(at, 1), h, :].rearrange("p a n -> p (a n)"),
                                        one(xc, row)[:, h * ROWTOK:(h + 1) * ROWTOK])
                return last

            def sample_stats(s):
                for slot in range(4):
                    if s == 0:
                        dve.wait_ge(first_loaded[slot], 16)
                    else:
                        dve.wait_ge(x_loaded, 16 * WROWS)
                    last = row_stats(x_stats, slot, s * WROWS + slot)
                last.then_inc(x_stats_done, 1)

            def step(instruction, norm, number):
                instruction.then_inc(norm_dve, 1)
                dve.wait_ge(norm_dve, norm * NORM_STEPS + number)

            def norm_moments(norm, stats, samples):
                for s in range(samples):
                    for h in range(HALVES):
                        last = dve.bn_aggr(moments[:, s * HALVES + h, :], stats[:, s * WROWS:(s + 1) * WROWS, h, :])
                step(last, norm, 1)

            def norm_means(norm, first, width, averages):
                wait(dve, norm_ready, norm)
                dve.wait_ge(norm_pe, norm * 2 + 1)
                dve.tensor_scalar(neg_mean[:, bass.ds(first, width)], averages[:, 0:width], -1.0, None, ALU.mult)
                step(dve.tensor_tensor(tiny[0][:, 0:width], moments[:, 0:width, 0], averages[:, 0:width], ALU.subtract), norm, 2)

            def norm_spreads(norm, width):
                step(dve.tensor_tensor(tiny[1][:, 0:width], tiny[0][:, 0:width], tiny[0][:, 0:width], ALU.mult), norm, 3)
                step(dve.tensor_tensor(tiny[2][:, 0:width], tiny[1][:, 0:width], moments[:, 0:width, 1], ALU.add), norm, 4)

            def norm_variances(norm, width, averages):
                dve.wait_ge(norm_pe, norm * 2 + 2)
                step(dve.tensor_scalar(tiny[3][:, 0:width], averages[:, NORMS:NORMS + width], EPS, 0.5, ALU.add, ALU.mult),
                     norm, 5)
                dve.tensor_scalar(root_guess[:, 0:width], tiny[3][:, 0:width].bitcast(i32), -0.5, float(0x5f3759df - (1 << 22)),
                                  ALU.mult, ALU.add).then_inc(norm_dve, 1)

            sample_stats(0)
            dve.wait_ge(x_stats_done, 1)
            norm_moments(0, x_stats, 1)
            norm_means(0, 0, HALVES, free_averages)
            norm_spreads(0, HALVES)
            norm_variances(0, HALVES, free_averages)
            norm_roots(dve, root_dve, 0, 0, 0, HALVES)
            for n, (first, end, scale) in enumerate(W_SCALES):
                dve.wait_ge(setup_act, n + 1)
                last = dve.scalar_tensor_tensor(w_lo[:, :, first:end], w_raw[:, :, first:end], scale,
                                                w_hi[:, :, first:end].bitcast(f32), ALU.mult, ALU.subtract)
            last.then_inc(setup_dve, 1)
            dve.wait_ge(setup_dve, 4)
            dve.wait_ge(setup_pe, 1)
            for e in range(2):
                half = slice(e * WS, (e + 1) * WS)
                last = dve.tensor_copy(bias_sum[half, 0, :].rearrange("p (g i) -> p g i", i=WS),
                                       pv_ps[half, :, :].rearrange("p b (n h) -> p h (b n)", h=HEADS)[:, e:HEADS:2, :])
            last.then_inc(setup_dve, 1)

            def low_with_bias(flat, first):
                for h in range(HALVES):
                    tok = slice(h * ROWTOK, (h + 1) * ROWTOK)
                    last = dve.scalar_tensor_tensor(flat[:, 1, tok], proj_ps[:, first // 2, tok],
                                                    b_cols[:, first + h:first + h + 1], flat[:, 0, tok], ALU.add, ALU.subtract)
                return last

            def q_split(slot, done, spread=0):
                dve.wait_ge(q_flat_done, done)
                wait(dve, q_spread[1 - slot], spread)
                low_with_bias(q_flat, 0).then_inc(q_lo_done, 1)
                for g in range(QUADS):
                    rows = slice(32 * g, 32 * g + 32)
                    last = dve.tensor_copy(q_hi[slot][rows, :, :, g, :].rearrange("p h w i -> p (h w) i"),
                                           q_flat[rows, 0, :].rearrange("p (n i) -> p n i", i=WS))
                last.then_inc(q_hi_done, 1)

            def k_split(slot, done):
                dve.wait_ge(k_flat_done, done)
                wait(dve, k_lo_done, done - 1)
                low_with_bias(k_flat, HALVES).then_inc(k_ps_read, 1)
                for part, (buf, spread) in enumerate(((k_hi[slot], k_hi_done), (k_lo[slot], k_lo_done))):
                    if part == 1:
                        dve.wait_ge(k_ps_read, done)
                    for e in range(2):
                        last = dve.tensor_scalar(buf[:, :, :, e, :].rearrange("p h w j -> p (h w) j"),
                                                 k_flat[:, part, :].rearrange("p (n j) -> p n j", j=WS),
                                                 parity_mask[:, e:e + 1], None, ALU.mult)
                    last.then_inc(spread, 1)

            def v_low(slot, done):
                dve.wait_ge(v_hi_done, done)
                for p in range(2):
                    for w in range(2):
                        for e in range(2):
                            rows = slice(e * WS, (e + 1) * WS)
                            last = dve.tensor_tensor(v_lo[2 * slot + p][rows, :, w, :, e, 0:D], v_part(p, w, e),
                                                     v_hi[2 * slot + p][rows, :, w, :, e, 0:D], ALU.subtract)
                last.then_inc(v_lo_done, 1)

            def maxima(n, p):
                dve.wait_ge(max_ps_done, n + 1)
                dve.tensor_reduce(neg_max[:, :], max_ps[:, :, :].rearrange("p w (n j) -> p (w n) j", j=WS), AX.X, ALU.max,
                                  negate=True).then_inc(neg_max_done, 1)
                dve.wait_ge(neg_max_done, n + 1)
                dve.tensor_copy(max_split[p][:, 0:16], neg_max[:, :]).then_inc(max_hi_done, 1)
                dve.wait_ge(max_hi_done, n + 1)
                dve.tensor_tensor(max_split[p][:, 16:32], neg_max[:, :], max_split[p][:, 0:16], ALU.subtract)\
                    .then_inc(max_split_done, 1)

            def attention_out(m, k, beside=None):
                dve.wait_ge(pv_ps_done, m + 1)
                if beside:
                    beside()
                wait(dve, attn_turned, m - 1)
                heads = pv_ps[:, :, 0:2 * WIN_N].rearrange("p h (w n d) -> p h w n d", w=2, d=D + 1)
                dve.reciprocal(recip[:, :, :, :], heads[:, :, :, :, D]).then_inc(recip_done, 1)
                dve.wait_ge(recip_done, m + 1)
                for w in range(2):
                    rows = slice(w * WS, (w + 1) * WS)
                    last = dve.tensor_tensor(attn[k % 2][rows, :, :, :], heads[rows, :, w, :, 0:D],
                                             recip[rows, :, w, :].unsqueeze(3).to_broadcast([WS, HALVES, 2 * QUADS, D]),
                                             ALU.mult)
                last.then_inc(attn_done, 1)

            dve.wait_ge(const_step, 8)
            q_split(0, 1)
            k_split(0, 1)
            v_low(0, 1)
            maxima(0, 0)
            dve.wait_ge(setup_act, 8)
            dve.tensor_tensor(b_row[32:33, :], b_raw[32:33, :], b_row[32:33, :].bitcast(f32), ALU.subtract)
            for v in range(4):
                dve.wait_ge(setup_act, 9 + v)
                last = dve.tensor_tensor(bias_lo[:, v, :], bias_sum[:, v, :], bias_hi[:, v, :].bitcast(f32), ALU.subtract)
            last.then_inc(setup_dve, 1)
            dve.wait_ge(const_step, 10)

            def pair(n, row, k, s):
                p = k % 2
                nxt = (k // 2 + 1) % 2
                norm, first, width, stage = norm_beside(s, k)
                if k == 0 and not is_first(n, 1) and has_sample(s, 1):
                    dve.wait_ge(x_loaded, row * 16 + WROWS * 16)
                    row_stats(x_stats, WROWS - 1, row + (2 * WROWS - 1)).then_inc(x_stats_done, 1)
                if k == 0 and has_sample(s, 1) and not is_first(n, 1):
                    dve.wait_ge(x_stats_done, s + 2)
                if not is_last_row(row):
                    if p == 0:
                        q_split(nxt, row + 2, times_slots(n, k, 64))
                        k_split(nxt, row + 2)
                    else:
                        v_low(nxt, row + 2)
                if is_first(n, 1):
                    sample_stats(1)
                    dve.wait_ge(x_stats_done, 2)
                if stage == -1 and has_sample(s, 1):
                    norm_moments(norm, x_stats, 1)
                if stage == 0 and not has_sample(s, 1):
                    dve.wait_ge(x1_stats_done, ROWS - WROWS)
                    norm_moments(norm, x1_stats, SAMPLES - 1)
                beside = None
                if stage == 0:
                    beside = lambda: norm_means(norm, first, width, spare_averages)
                if stage == 1:
                    beside = lambda: norm_variances(norm, width, spare_averages)
                if not is_first(n, 1):
                    attention_out(n - 1, (k - 1) % 4, beside)
                if not is_last_pair(n):
                    maxima(n + 1, 1 - p)
                if stage == 0:
                    norm_spreads(norm, width)
                if k > 1 and p == 1 and has_sample(s, 2):
                    dve.wait_ge(x_loaded, row * 16 + WROWS * 16)
                    row_stats(x_stats, k // 2 - 1, row + (2 * WROWS - 1))
                if p == 0 and not is_first(n, 4):
                    dve.wait_ge(x1_done, n - 2)
                    row_stats(x1_stats, row - 2, row - 2).then_inc(x1_stats_done, 1)

            run(dve, pair)
            attention_out(PAIRS - 1, 3)

            def lif_units(y):
                for t in range(SAMPLES):
                    m = y * SAMPLES + t
                    level = first_charge if t == 0 else charged[t % 2][:, :]
                    if t == 0:
                        dve.wait_ge(first_done, y + 1)
                    else:
                        dve.wait_ge(h_ps_done, m + 1)
                        wait(dve, spike_done, y * SAMPLES + (t - 1))
                        dve.wait_ge(reset_done, y * (SAMPLES - 1) + t)
                        dve.scalar_tensor_tensor(level, membrane[:, :], 1.0 - 1.0 / TAU, banks[t], ALU.mult, ALU.add)\
                           .then_inc(charge_done, 1)
                        dve.wait_ge(charge_done, y * (SAMPLES - 1) + t)
                    if t < SAMPLES - 1:
                        dve.scalar_tensor_tensor(membrane[:, :], level, 1.0, level,
                                                 ALU.is_lt, ALU.mult).then_inc(reset_done, 1)
                    dve.scalar_tensor_tensor(one(xc, y + t * WROWS), level, 1.0, one(xc, y + t * WROWS),
                                             ALU.is_ge, ALU.add)\
                       .then_inc(spike_done, 1)
                    if is_first(y, 1) and t == 0:
                        last = SAMPLES + 1
                        for back in (2, 1):
                            dve.wait_ge(x1_done, PAIRS + 2 - 2 * back)
                            row_stats(x1_stats, ROWS - back, ROWS - back).then_inc(x1_stats_done, 1)
                        dve.wait_ge(x1_stats_done, ROWS)
                        norm_moments(last, x1_stats[:, ROWS - WROWS:ROWS], 1)
                        norm_means(last, EARLY, HALVES, free_averages)
                        norm_spreads(last, HALVES)
                        norm_variances(last, HALVES, free_averages)

            over_y(dve, lif_units)

        @block.tensor
        def _(pe):
            pe.wait_ge(const_step, 4)

            def average_means(norm, width, averages):
                pe.wait_ge(norm_dve, norm * NORM_STEPS + 1)
                pe.matmul(averages[:, 0:width], group_avg[:, :], moments[:, 0:width, 0], start=True, stop=True).then_inc(norm_pe, 1)

            def average_variances(norm, width, averages):
                pe.wait_ge(norm_dve, norm * NORM_STEPS + 4)
                pe.matmul(averages[:, NORMS:NORMS + width], group_avg[:, :], tiny[2][:, 0:width], start=True, stop=True)\
                  .then_inc(norm_pe, 1)

            pe.wait_ge(const_step, 6)
            average_means(0, HALVES, free_averages)
            average_variances(0, HALVES, free_averages)
            pe.wait_ge(tab_loaded, 16 * WIN)
            for j in range(2):
                last = pe.matmul(pv_ps[:, j, :], flip[:, :], bias_raw[:, j * 512:(j + 1) * 512], start=True, stop=True)
            last.then_inc(setup_pe, 1)

            def project_channels(bank, first, high, low, bias=False):
                for h in range(HALVES):
                    dst = bank[:, h * ROWTOK:(h + 1) * ROWTOK]
                    cols = slice(first + h * 128, first + (h + 1) * 128)
                    if bias:
                        pe.matmul(dst, b_row[:, h * 128:(h + 1) * 128], ones_r[:, :], start=True, stop=False)
                    for c in range(HALVES):
                        tok = slice(c * ROWTOK, (c + 1) * ROWTOK)
                        pe.matmul(dst, w_hi[:, c, cols], high[:, tok], start=(c == 0 and not bias), stop=False)
                        pe.matmul(dst, w_hi[:, c, cols], low[:, tok], start=False, stop=False)
                        last = pe.matmul(dst, w_lo[:, c, cols], high[:, tok], start=False, stop=(c == HALVES - 1))
                return last

            def project_tokens(dst, tile, first, slot):
                cols = slice(first, first + C)
                for c in range(HALVES):
                    tok = slice(c * ROWTOK + tile * 128, c * ROWTOK + (tile + 1) * 128)
                    pe.matmul(dst, xn_hi[slot][:, tok], w_hi[:, c, cols], start=(c == 0), stop=False)
                    pe.matmul(dst, xn_hi[slot][:, tok], w_lo[:, c, cols], start=False, stop=False)
                    last = pe.matmul(dst, xn_lo[slot][:, tok], w_hi[:, c, cols], start=False, stop=(c == HALVES - 1))
                return last

            def project_q(slot, r):
                pe.wait_ge(xn_lo_done, r + 1)
                wait(pe, v_lo_done, r)
                project_channels(banks[6], 0, xn_hi[slot], xn_lo[slot]).then_inc(q_ps_done, 1)

            def project_k(slot, r):
                wait(pe, attn_kept, 2 * r - 4)
                project_channels(banks[7], C, xn_hi[slot], xn_lo[slot]).then_inc(k_ps_done, 1)

            def project_v(slot, r):
                pe.wait_ge(q_lo_done, r + 1)
                for p in range(2):
                    last = project_tokens(proj_ps[:, 0, p * C:(p + 1) * C], p, 2 * C, slot)
                last.then_inc(v_ps_done, 1)

            def variant(k, w):
                return 2 * (k // 2 == WROWS - 1) + (2 * (k % 2) + w == WCOLS - 1)

            def max_scores(m, row, k):
                slot = k // 2 % 2
                if k % 2 == 0:
                    pe.wait_ge(k_hi_done, row + 1)
                wait(pe, max_rows_done, m)
                for w in range(2):
                    pe.matmul(max_ps[:, w, :], ident_r[:, :], bias_q[:, variant(k, w), :], start=True, stop=False)
                    wx = 2 * (k % 2) + w
                    for h in range(HALVES):
                        for mid in range(2):
                            at = (2 * h + mid) * 128
                            last = pe.matmul(max_ps[:, w, at:at + 128],
                                             q_hi[slot][:, h, wx, 2 * mid:2 * mid + 2, :].rearrange("p q i -> p (q i)"),
                                             k_hi[slot][:, h, wx, :, :].rearrange("p e j -> p (e j)"),
                                             start=False, stop=(h == 1 and mid == 1))
                last.then_inc(max_ps_done, 1)

            def scores(n, row, k):
                slot, p = k // 2 % 2, k % 2
                if p == 0:
                    pe.wait_ge(k_lo_done, row + 1)
                    pe.wait_ge(q_spread[slot], times_slots(n, k, 64))
                for w in range(2):
                    wx = 2 * p + w
                    wait(pe, p_hi_done, n * 2 + (w - 1))
                    v = variant(k, w)
                    pe.matmul(score_ps[:, w, :], ident_r[:, :], bias_hi[:, v, :], start=True, stop=False)
                    pe.matmul(score_ps[:, w, :], ident_r[:, :], bias_lo[:, v, :], start=False, stop=False)
                    for h in range(HALVES):
                        dst = score_ps[:, w, h * 256:(h + 1) * 256]
                        at_q = (h * WCOLS + wx) * WS
                        high = q_hi[slot][:, h, wx, :, :].rearrange("p q i -> p (q i)")
                        for keys, queries in ((k_hi, high), (k_hi, q_lo[slot][:, :, at_q:at_q + WS]), (k_lo, high)):
                            pe.matmul(dst, keys[slot][:, h, wx, :, :].rearrange("p e j -> p (e j)"), queries,
                                      start=False, stop=False)
                    if w == 0:
                        turn_maxima(n, p)
                pe.wait_ge(max_rows_done, n + 1)
                for w in range(2):
                    for b in range(4):
                        last = pe.matmul(score_ps[:, w, b * 128:(b + 1) * 128], pick_max[:, 4 * w + b, :], max_rows[p][:, :],
                                         start=False, stop=(b == 3))
                    last.then_inc(score_ps_done, 1)

            def turn_maxima(n, p):
                pe.wait_ge(max_split_done, n + 1)
                pe.transpose(max_ps[:, 0, :].bitcast(bf16)[0:32, 0:128], max_split[p][:, :], ident_b[:, :])\
                  .then_inc(max_turned, 1)

            def weigh_values(m, row, k, beside=None):
                p = k % 2
                pe.wait_ge(p_lo_done, m * 2 + 2)
                if p == 0:
                    pe.wait_ge(v_lo_done, row + 1)
                wait(pe, attn_done, m)
                if beside:
                    beside()
                for h in range(HALVES):
                    cols = pv_ps[:, h, 0:2 * WIN_N].rearrange("p (w g n) -> p w g n", w=2, g=QUADS)
                    for g in range(QUADS):
                        for at, (pp, vv) in enumerate(((p_hi, v_hi), (p_hi, v_lo), (p_lo, v_hi))):
                            last = pe.matmul(cols[:, :, g, :], pp[p][:, h * QUADS + g, :, :].rearrange("p w i -> p (w i)"),
                                             vv[k][:, h, :, g, :, :].rearrange("p w e d -> p w (e d)"),
                                             start=(at == 0), stop=(at == 2))
                last.then_inc(pv_ps_done, 1)

            def turn_attention(m, p):
                pe.wait_ge(attn_done, m + 1)
                wait(pe, attn_kept, m)
                tokens = attn[p][:, :, :, :].rearrange("p h n d -> p (h n d)")
                for h in range(HALVES):
                    last = pe.transpose(proj_ps[:, 1, h * 128:(h + 1) * 128], tokens[:, h * 128:(h + 1) * 128], ident[:, :])
                last.then_inc(attn_turned, 1)

            pe.wait_ge(setup_dve, 4)
            project_q(0, 0)
            project_k(0, 0)
            project_v(0, 0)
            pe.wait_ge(setup_dve, 5)
            for v in range(4):
                wait(pe, masked, v)
                if v >= 2:
                    pe.wait_ge(setup_act, 2 + v)
                for j in range(4):
                    last = pe.transpose(banks[4 + v % 2][:, j * 128:(j + 1) * 128], bias_sum[:, v, j * 128:(j + 1) * 128],
                                        ident[:, :])
                last.then_inc(setup_pe, 1)
            pe.wait_ge(setup_act, 7)
            max_scores(0, 0, 0)

            def unit_products(m, t):
                pe.wait_ge(xn_lo_done, m + (ROWS + 1))
                project_channels(banks[t], 3 * C, unit_hi[t % 4], unit_lo[t % 4], True).then_inc(h_ps_done, 1)

            def pair(n, row, k, s):
                p = k % 2
                nxt = (k // 2 + 1) % 2
                if not is_last_row(row):
                    if p == 0:
                        project_q(nxt, row + 1)
                        project_k(nxt, row + 1)
                    else:
                        project_v(nxt, row + 1)
                if is_first(n, 1):
                    pe.wait_ge(setup_act, SETUP_ACT)
                    pe.wait_ge(setup_dve, SETUP_DVE)
                scores(n, row, k)
                norm, _, width, stage = norm_beside(s, k)
                beside = None
                if stage == 0:
                    beside = lambda: average_means(norm, width, spare_averages)
                if stage == 1:
                    beside = lambda: average_variances(norm, width, spare_averages)
                if not is_first(n, 1):
                    weigh_values(n - 1, row if p else row - 1, (k - 1) % 4, beside)
                if not is_last_pair(n):
                    max_scores(n + 1, row + 1 if p else row, (k + 1) % BODY)
                if p == 0 and not is_last_row(row):
                    pe.wait_ge(k_ps_read, row + 2)
                if not is_first(n, 2):
                    turn_attention(n - 2, p)
                if is_last_pair(n):
                    unit_products(0, 0)

            run(pe, pair)
            weigh_values(PAIRS - 1, ROWS - 1, 3)
            turn_attention(PAIRS - 2, 0)
            turn_attention(PAIRS - 1, 1)

            def lif_units(y):
                for t in range(SAMPLES):
                    m = y * SAMPLES + t
                    wait(pe, spike_done, m - 7)
                    if is_first(y, 1) and t == 6:
                        pe.wait_ge(norm_dve, (SAMPLES + 1) * NORM_STEPS + 5)
                        pe.wait_ge(attn_kept, PAIRS)
                    if not (is_first(y, 1) and t == 0):
                        unit_products(m, t)
                    if is_first(y, 1) and t == 1:
                        average_means(SAMPLES + 1, HALVES, free_averages)
                        average_variances(SAMPLES + 1, HALVES, free_averages)

            over_y(pe, lif_units)


def kernel(**inputs):
    import numpy as _np
    import concourse.bacc as _bacc
    from concourse import mybir as _mybir
    from concourse.bass_utils import run_bass_kernel_spmd as _run

    x = inputs["x"]
    samples, height, width, channels = x.shape
    rows, cols, halves = height // 8, width // 8, channels // 128
    tiled = _np.asarray(x).reshape(samples, rows, 8, cols, 8, halves, 128).transpose(0, 6, 1, 5, 3, 2, 4)
    laid_out = {
        "x": tiled.reshape(samples, 128, rows, halves * cols * 64),
        "qkv_w": _np.asarray(inputs["L0_conv_qkv_w"]).T,
        "qkv_b": _np.asarray(inputs["L0_conv_qkv_b"]).reshape(-1, 128).T,
        "bias_table": inputs["L0_conv_bias_table"],
        "lif_w": _np.asarray(inputs["L1_conv_W"]).T,
        "lif_b": inputs["L1_conv_b"],
    }
    nc = _bacc.Bacc("TRN2", target_bir_lowering=False, num_devices=1)
    arrays, args = {}, []
    for name, array in laid_out.items():
        a = _np.ascontiguousarray(array)
        arrays[f"in_{name}_dram"] = a
        args.append(nc.dram_tensor(f"in_{name}_dram", a.shape, _mybir.dt.from_np(a.dtype), kind="ExternalInput").ap())
    shape = arrays["in_x_dram"].shape
    args.append(nc.dram_tensor("out_0_dram", shape, _mybir.dt.float32, kind="ExternalOutput").ap())
    swin_attention_then_lif_kernel(nc, x.shape, *args)
    r = _run(nc, [arrays], core_ids=[0])
    out = r.results[0]["out_0_dram"].reshape(samples, 128, rows, halves, cols, 8, 8)
    return out.transpose(0, 2, 5, 4, 6, 3, 1).reshape(samples, height, width, channels)
```
